# Optimizing a Trainium2 kernel written in Bass

```python
import numpy as np
import jax
import jax.numpy as jnp

def _softmax(x, axis=-1):
    return jax.nn.softmax(x, axis=axis)

def _gelu(x):
    return jax.nn.gelu(x, approximate=True)

def _silu(x):
    return jax.nn.silu(x)

def _sigmoid(x):
    return jax.nn.sigmoid(x)

def _layernorm(x, axis=-1, eps=1e-05):
    m = jnp.mean(x, axis=axis, keepdims=True)
    v = jnp.var(x, axis=axis, keepdims=True)
    return (x - m) / jnp.sqrt(v + eps)

def _scatter_add(tgt, idx, src, axis=0):
    return tgt.at[idx].add(src)

def _segment_sum(src, seg, n):
    return jax.ops.segment_sum(src, seg, n)
kernel_name = 'mk_adaln_ffn_d2_seqx_r8_2c241c'

def setup_inputs(seed: int=0):
    np.random.seed(seed)
    _w = jnp.asarray

    def _rec_inputs():
        import jax
        import jax.numpy as jnp
        _rk = jax.random.key(seed)
        x = -5.722e-05 + 0.9998 * jax.random.normal(jax.random.fold_in(_rk, 1), (32, 128, 128), jnp.float32)
        _lenS = 128 - jax.random.randint(jax.random.fold_in(_rk, 7), (32,), 0, max(1, 128 // 4) + 1, jnp.int32)
        _lenS2 = 128 - jax.random.randint(jax.random.fold_in(_rk, 8), (32,), 0, max(1, 128 // 4) + 1, jnp.int32)
        cond_1024 = -0.00499425 + 1.0058 * jax.random.normal(jax.random.fold_in(_rk, 11), (32, 128), jnp.float32)
        return (x, cond_1024)
    x, cond_1024 = _rec_inputs()

    def _L0_cond_setup():
        import jax, jax.numpy as jnp
        import numpy as np
        key = jax.random.key(seed)
        k1, k2 = jax.random.split(key)
        B, S, D = (32, 256, 128)
        query = jax.random.normal(k1, (B, D), dtype=jnp.float32)
        values = jax.random.normal(k2, (B, S, D), dtype=jnp.float32)
        return {'query': query, 'values': values}
    _L0_cond_all = _L0_cond_setup()
    _L0_cond_in = {k: v for k, v in _L0_cond_all.items() if k in ()}
    del _L0_cond_all

    def _L0_ffn_setup():
        import jax, jax.numpy as jnp
        import numpy as np
        B, S, D, E, K = (2, 256, 128, 8, 2)
        H = 4 * D
        key = jax.random.key(seed)
        ks = jax.random.split(key, 6)
        x = jax.random.normal(ks[0], (B, S, D), dtype=jnp.float32)
        lim_g = np.sqrt(6.0 / (D + E)).astype(np.float32)
        W_gate = jax.random.uniform(ks[1], (D, E), minval=-lim_g, maxval=lim_g, dtype=jnp.float32)
        lim1 = np.sqrt(1.0 / D).astype(np.float32)
        lim2 = np.sqrt(1.0 / H).astype(np.float32)
        W1 = jax.random.uniform(ks[2], (E, D, H), minval=-lim1, maxval=lim1, dtype=jnp.float32)
        b1 = jax.random.uniform(ks[3], (E, H), minval=-lim1, maxval=lim1, dtype=jnp.float32)
        W2 = jax.random.uniform(ks[4], (E, H, D), minval=-lim2, maxval=lim2, dtype=jnp.float32)
        b2 = jax.random.uniform(ks[5], (E, D), minval=-lim2, maxval=lim2, dtype=jnp.float32)
        return {'x': x, 'W_gate': W_gate, 'W1': W1, 'b1': b1, 'W2': W2, 'b2': b2}
    _L0_ffn_all = _L0_ffn_setup()
    _L0_ffn_in = {k: v for k, v in _L0_ffn_all.items() if k in ('W_gate', 'W1', 'b1', 'W2', 'b2')}
    del _L0_ffn_all

    def _L1_cond_setup():
        import jax, jax.numpy as jnp
        import numpy as np
        INPUT_DIM = 128
        LATENT_DIM = 128
        key = jax.random.key(seed)
        ks = jax.random.split(key, 8)
        B, T = (64, 64)
        concat_dim = INPUT_DIM + LATENT_DIM
        s = lambda fan_in: 1.0 / np.sqrt(fan_in)
        return {'x': jax.random.normal(ks[0], (B, T, INPUT_DIM), dtype=jnp.float32), 'h0': jax.random.normal(ks[1], (B, LATENT_DIM), dtype=jnp.float32), 'w_W': jax.random.uniform(ks[2], (concat_dim, 2 * LATENT_DIM), jnp.float32, -s(concat_dim), s(concat_dim)), 'w_b': jax.random.uniform(ks[3], (2 * LATENT_DIM,), jnp.float32, -s(concat_dim), s(concat_dim)), 'wx_W': jax.random.uniform(ks[4], (INPUT_DIM, LATENT_DIM), jnp.float32, -s(INPUT_DIM), s(INPUT_DIM)), 'wx_b': jax.random.uniform(ks[5], (LATENT_DIM,), jnp.float32, -s(INPUT_DIM), s(INPUT_DIM)), 'wh_W': jax.random.uniform(ks[6], (LATENT_DIM, LATENT_DIM), jnp.float32, -s(LATENT_DIM), s(LATENT_DIM)), 'wh_b': jax.random.uniform(ks[7], (LATENT_DIM,), jnp.float32, -s(LATENT_DIM), s(LATENT_DIM))}
    _L1_cond_all = _L1_cond_setup()
    _L1_cond_in = {k: v for k, v in _L1_cond_all.items() if k in ('w_W', 'w_b', 'wx_W', 'wx_b', 'wh_W', 'wh_b')}
    del _L1_cond_all

    def _L1_ffn_setup():
        import jax, jax.numpy as jnp
        import numpy as np
        TOP_K = 2

        def _mlp(x, w_fc, w_proj):
            return jnp.square(jax.nn.relu(x @ w_fc.T)) @ w_proj.T
        key = jax.random.key(seed)
        ks = jax.random.split(key, 6)
        B, S, D, E = (4, 256, 128, 8)
        d_ff = 4 * D
        x = jax.random.normal(ks[0], (B, S, D), dtype=jnp.float32)
        router_w = jax.random.normal(ks[1], (E, D), dtype=jnp.float32) * 0.02
        w_fc = jax.random.normal(ks[2], (E, d_ff, D), dtype=jnp.float32) * 0.02
        w_proj = jax.random.normal(ks[3], (E, D, d_ff), dtype=jnp.float32) * 0.02
        shared_fc = jax.random.normal(ks[4], (d_ff, D), dtype=jnp.float32) * 0.02
        shared_proj = jax.random.normal(ks[5], (D, d_ff), dtype=jnp.float32) * 0.02
        return {'x': x, 'router_w': router_w, 'w_fc': w_fc, 'w_proj': w_proj, 'shared_fc': shared_fc, 'shared_proj': shared_proj}
    _L1_ffn_all = _L1_ffn_setup()
    _L1_ffn_in = {k: v for k, v in _L1_ffn_all.items() if k in ('router_w', 'w_fc', 'w_proj', 'shared_fc', 'shared_proj')}
    del _L1_ffn_all
    return {'x': x, 'cond_1024': cond_1024, 'L0_ffn_W_gate': _L0_ffn_in['W_gate'], 'L0_ffn_W1': _L0_ffn_in['W1'], 'L0_ffn_b1': _L0_ffn_in['b1'], 'L0_ffn_W2': _L0_ffn_in['W2'], 'L0_ffn_b2': _L0_ffn_in['b2'], 'L1_cond_w_W': _L1_cond_in['w_W'], 'L1_cond_w_b': _L1_cond_in['w_b'], 'L1_cond_wx_W': _L1_cond_in['wx_W'], 'L1_cond_wx_b': _L1_cond_in['wx_b'], 'L1_cond_wh_W': _L1_cond_in['wh_W'], 'L1_cond_wh_b': _L1_cond_in['wh_b'], 'L1_ffn_router_w': _L1_ffn_in['router_w'], 'L1_ffn_w_fc': _L1_ffn_in['w_fc'], 'L1_ffn_w_proj': _L1_ffn_in['w_proj'], 'L1_ffn_shared_fc': _L1_ffn_in['shared_fc'], 'L1_ffn_shared_proj': _L1_ffn_in['shared_proj']}

def reference(x, cond_1024, L0_ffn_W_gate, L0_ffn_W1, L0_ffn_b1, L0_ffn_W2, L0_ffn_b2, L1_cond_w_W, L1_cond_w_b, L1_cond_wx_W, L1_cond_wx_b, L1_cond_wh_W, L1_cond_wh_b, L1_ffn_router_w, L1_ffn_w_fc, L1_ffn_w_proj, L1_ffn_shared_fc, L1_ffn_shared_proj):
    import jax
    import jax.numpy as jnp

    def _L0_cond_ref(query, values):
        import jax, jax.numpy as jnp
        import numpy as np
        D = query.shape[-1]
        weights = jnp.einsum('bd,bsd->bs', query, values) / jnp.sqrt(jnp.asarray(D, query.dtype))
        weights = jax.nn.softmax(weights, axis=0)
        return values * weights[..., None]

    def _L0_ffn_ref(x, W_gate, W1, b1, W2, b2):
        import jax, jax.numpy as jnp
        import numpy as np
        B, S, D, E, K = (2, 256, 128, 8, 2)
        H = 4 * D
        gate = jnp.einsum('bsd,de->bse', x, W_gate)
        kth = jax.lax.top_k(gate, K)[0][..., -1:]
        mask = jax.nn.softmax(jnp.where(gate >= kth, gate, -jnp.inf), axis=-1)
        h = jax.nn.relu(jnp.einsum('bsd,edh->bseh', x, W1) + b1)
        y = jnp.einsum('bseh,ehd->bsed', h, W2) + b2
        return (y * mask[..., None]).mean(axis=-2)

    def _L1_cond_ref(x, h0, w_W, w_b, wx_W, wx_b, wh_W, wh_b):
        import jax, jax.numpy as jnp
        import numpy as np
        INPUT_DIM = 128
        LATENT_DIM = 128
        xT = jnp.swapaxes(x, 0, 1)

        def step(h, x_t):
            fused = jax.nn.sigmoid(jnp.concatenate([x_t, h], axis=-1) @ w_W + w_b)
            hidden_state, output_state = jnp.split(fused, 2, axis=-1)
            memory_state = x_t @ wx_W + wx_b + hidden_state * (h @ wh_W + wh_b)
            h_new = output_state * h + (1.0 - output_state) * jnp.tanh(memory_state)
            return (h_new, h_new)
        _, hs = jax.lax.scan(step, h0, xT)
        return jnp.swapaxes(hs, 0, 1)

    def _L1_ffn_ref(x, router_w, w_fc, w_proj, shared_fc, shared_proj):
        import jax, jax.numpy as jnp
        import numpy as np
        TOP_K = 2

        def _mlp(x, w_fc, w_proj):
            return jnp.square(jax.nn.relu(x @ w_fc.T)) @ w_proj.T
        B, S, D = x.shape
        E = router_w.shape[0]
        T = B * S
        flat = x.reshape(T, D)
        logits = flat @ router_w.T
        probs = jax.nn.softmax(logits.astype(jnp.float32), axis=-1)
        topk_p, topk_i = jax.lax.top_k(probs, TOP_K)
        topk_w = (topk_p / jnp.maximum(topk_p.sum(-1, keepdims=True), 1e-09)).astype(flat.dtype)
        combine = jnp.zeros((T, E), dtype=flat.dtype)
        combine = combine.at[jnp.arange(T)[:, None], topk_i].add(topk_w)
        out = jnp.zeros_like(flat)
        for e in range(E):
            out = out + _mlp(flat, w_fc[e], w_proj[e]) * combine[:, e:e + 1]
        out = out + _mlp(flat, shared_fc, shared_proj)
        return out.reshape(B, S, D)
    x = x + _L0_ffn_ref(_L0_cond_ref(cond_1024, x), L0_ffn_W_gate, L0_ffn_W1, L0_ffn_b1, L0_ffn_W2, L0_ffn_b2)
    x = x + _L1_ffn_ref(_L1_cond_ref(x, cond_1024, L1_cond_w_W, L1_cond_w_b, L1_cond_wx_W, L1_cond_wx_b, L1_cond_wh_W, L1_cond_wh_b), L1_ffn_router_w, L1_ffn_w_fc, L1_ffn_w_proj, L1_ffn_shared_fc, L1_ffn_shared_proj)
    return x

_drawn_inputs = setup_inputs


def setup_inputs(seed=0):
    import zlib

    import numpy as np

    out = dict(_drawn_inputs(seed))
    spreads = {}
    factors = {'cond_1024': 8.0,
     'L0_ffn_W_gate': 8.0,
     'L0_ffn_W1': 8.0,
     'L0_ffn_b1': 8.0,
     'L0_ffn_W2': 8.0,
     'L0_ffn_b2': 8.0,
     'L1_cond_w_W': 8.0,
     'L1_cond_w_b': 8.0,
     'L1_cond_wx_W': 8.0,
     'L1_cond_wx_b': 8.0,
     'L1_cond_wh_W': 8.0,
     'L1_cond_wh_b': 8.0,
     'L1_ffn_router_w': 8.0,
     'L1_ffn_w_fc': 8.0,
     'L1_ffn_w_proj': 8.0,
     'L1_ffn_shared_fc': 8.0,
     'L1_ffn_shared_proj': 8.0}
    for name, (base, spread) in spreads.items():
        noise = np.random.default_rng([zlib.crc32(name.encode()), seed]).standard_normal(out[name].shape)
        drawn = base * np.exp(spread * noise) if base else spread * noise
        out[name] = jnp.asarray(drawn.astype(out[name].dtype))
    for name, factor in factors.items():
        out[name] = (out[name] * factor).astype(out[name].dtype)
    return out
```

```python
from contextlib import ExitStack

import concourse.bass as bass
from concourse import mybir

F32 = mybir.dt.float32
F32R = mybir.dt.float32r
ALU = mybir.AluOpType
ACT = mybir.ActivationFunctionType
AX = mybir.AxisListType

D = 128
SEQ = 128
BATCH = 32
STEPS = 16
N = STEPS * BATCH
BLOCKS = SEQ // STEPS
EXPERTS = 8
CHUNKS = 4
HALF = STEPS // 2
TOK = N // D
LAG = 4
RING = 4
L0, L1 = 0, 1
GROUPS = {L0: EXPERTS, L1: EXPERTS + 1}
TILES = {q: GROUPS[q] * CHUNKS for q in (L0, L1)}
STAGE = 2
MASKS = 4
W_L0 = 2 * GROUPS[L0]
W_ALL = 2 * (GROUPS[L0] + GROUPS[L1])

SMALL = {}
_at = 0
for _name, _width in (("cond", BATCH), ("b1", EXPERTS * CHUNKS), ("b2", EXPERTS), ("bx", 1), ("bh", 1),
                      ("gate", EXPERTS), ("router", EXPERTS), ("rec", 3 * D), ("ident", D),
                      ("ones", D), ("lower", EXPERTS * EXPERTS), ("pick", 2)):
    SMALL[_name] = (_at, _at + _width)
    _at += _width
SMALL_COLS = _at


def lo_on_pool(q, j):
    return j % 2 == 1


class Pass:

    def __init__(self, k, l1, rec, l0, carry, flush, before):
        self.k, self.l1, self.rec, self.l0 = k, l1, rec, l0
        self.carry = carry
        self.flush = flush
        self.before = before
        self.block = {L0: k + 1, L1: k - 1}
        self.tiles = [(L1, j) for j in range(TILES[L1] if l1 else 0)] + [(L0, j) for j in range(TILES[L0] if l0 else 0)]
        self.n = len(self.tiles)
        self.slots = self.n + (LAG + 3 if flush else 0)
        self.first_l0 = TILES[L1] if l1 else 0
        full = l1
        self.logits1, self.mask1a, self.exp1, self.mask1b, self.turn1, self.evac1 = 0, 1, 2, 5, 8, 9
        self.x1_split, self.xproj, self.xw = (6, 9, 10) if full else (0, 0, 0)
        (self.prod, self.wdot, self.shift, self.exp_w, self.scale, self.v_split, self.gates,
         self.mask0a, self.exp0, self.mask0b, self.turn0, self.evac0) = \
            (11, 13, 14, 15, 16, 19, 20, 22, 23, 24, 26, 27) if full else (0,) * 12
        self.copy1 = 0 if not l1 else self.n + LAG + 2 if not l0 else self.first_l0 + LAG + 3
        start, stride = (10, 3.7) if (l1 and l0) else (10, 1.75) if l1 else (1, 1.9)
        self.hs_split = int(start + (STEPS - 1) * stride) + 3
        if not flush:
            self.hs_split = min(self.hs_split, self.n - 1)
        self.step_at = {int(start + u * stride): u for u in range(STEPS)} if rec else {}

    def tile(self, i):
        if i >= self.n or (i < 0 and not self.carry):
            return None
        return self.any_tile(i)

    def any_tile(self, i):
        if i >= 0:
            q, j = self.tiles[i]
            return q, j, self.block[q]
        if self.before is None:
            return None
        return self.before, TILES[self.before] + i, (self.k if self.before == L0 else self.k - 2)


def first_passes():
    return [Pass(-1, False, False, True, False, True, None), Pass(0, False, True, True, False, False, L0)]


def loop_pass(k):
    return Pass(k, True, True, True, True, False, L0)


def last_passes():
    return [Pass(BLOCKS - 1, True, True, False, True, True, L0), Pass(BLOCKS, True, False, False, False, True, L1)]


def run_passes(engine, body):
    for it in first_passes():
        body(it)
    with engine.Fori(1, BLOCKS - 1) as k:
        body(loop_pass(k))
    for it in last_passes():
        body(it)


def tile_count(t):
    q, j, block = t
    return block * TILES[q] + (j + 1)


def lo_count(t):
    q, j, block = t
    mine = lo_on_pool(q, j)
    per = sum(lo_on_pool(q, i) == mine for i in range(TILES[q]))
    return block * per + sum(lo_on_pool(q, i) == mine for i in range(j + 1))


def w_slots(it):
    out = {}
    if it.l0 and not it.rec:
        for c in range(W_L0):
            out.setdefault(0 if c < 2 else CHUNKS * (c // 2 - 1) + 2 * (c % 2), []).append(c)
    elif it.l0 and not it.l1:
        for c in range(W_L0, W_ALL):
            out.setdefault(1 + (c - W_L0) * (TILES[L0] - 4) // (W_ALL - W_L0), []).append(c)
    return out


class Chain:

    def __init__(self, engine, sem, steps):
        self.engine, self.sem, self.steps = engine, sem, steps

    def begin(self, block):
        self.base, self.n = block * self.steps, 0

    def __call__(self, instruction):
        self.n += 1
        assert self.n <= self.steps
        instruction.then_inc(self.sem, 1)
        self.engine.wait_ge(self.sem, self.base + self.n)


def build(nc, x_dram, weights_dram, small_dram, xp_dram, bias_dram, mask_dram, out_dram):
    with ExitStack() as ctx:
        def sb(name, shape, dt=F32):
            return ctx.enter_context(nc.sbuf_tensor(name, shape, dt))

        def bank(name):
            return ctx.enter_context(nc.psum_tensor(name, [D, N], F32))

        def sem(name):
            return ctx.enter_context(nc.semaphore(name))

        def per_layer(name):
            return {q: sem(f"{name}{q}") for q in (L0, L1)}

        first_hi = {q: sb(f"first_hi{q}", [D, GROUPS[q], N], F32R) for q in (L0, L1)}
        first_lo = {q: sb(f"first_lo{q}", [D, GROUPS[q], N], F32R) for q in (L0, L1)}
        second_hi = {q: sb(f"second_hi{q}", [D, GROUPS[q], N], F32R) for q in (L0, L1)}
        second_lo = {q: sb(f"second_lo{q}", [D, GROUPS[q], N], F32R) for q in (L0, L1)}
        small = sb("small", [D, SMALL_COLS])
        xp_hi = sb("xp_hi", [D, 3 * D], F32R)
        xp_lo = sb("xp_lo", [D, 3 * D], F32R)
        bias_pair = sb("bias_pair", [2, 2 * D], F32R)
        ones_pair = sb("ones_pair", [2, BATCH], F32R)

        x_t = sb("x_t", [D, N])
        v = sb("v", [D, N])
        in0_hi = sb("in0_hi", [D, N], F32R)
        in0_lo = sb("in0_lo", [D, N], F32R)
        x1 = sb("x1", [D, N])
        hs = sb("hs", [D, N])
        hs_hi = sb("hs_hi", [D, N], F32R)
        hs_lo = sb("hs_lo", [D, N], F32R)
        xw = sb("xw", [D, N])
        out1 = sb("out1", [D, N])
        hid = sb("hid", [D, RING, N])
        hid_hi = sb("hid_hi", [D, RING, N], F32R)
        hid_lo = sb("hid_lo", [D, RING, N], F32R)
        term = sb("term", [D, 2, N])
        mask_all = sb("mask_all", [D, MASKS, N])
        compare = sb("compare", [D, N])
        mask_t = compare[0:EXPERTS, :]

        stage = sb("stage", [D, STAGE, N])
        xp_raw = xw[:, 0:3 * D]
        bias_raw = hs[0:2, 0:2 * D]

        w_max = sb("w_max", [D, STEPS])
        w_sum = sb("w_sum", [D, STEPS])
        w_inv = sb("w_inv", [D, STEPS])
        g = {q: sb(f"g{q}", [D, TOK, EXPERTS]) for q in (L0, L1)}
        top = sb("top", [D, TOK, 8])
        kept = sb("kept", [D, TOK, EXPERTS])
        stat = {q: sb(f"stat{q}", [D, 4, TOK]) for q in (L0, L1)}
        mask = {q: sb(f"mask{q}", [D, TOK, EXPERTS]) for q in (L0, L1)}
        prob = sb("prob", [D, TOK, EXPERTS])
        rank = sb("rank", [D, TOK, EXPERTS])
        above, equal = (compare[:, N // 2 * a:N // 2 * (a + 1)].rearrange("p (t e j) -> p t e j", t=TOK, e=EXPERTS) for a in range(2))
        th_gates = sb("th_gates", [D, 2 * BATCH])
        memory = sb("memory", [D, BATCH])
        th_mem = sb("th_mem", [D, BATCH])
        keep_not = sb("keep_not", [D, BATCH])
        keep2 = sb("keep2", [D, BATCH])

        z = [bank("z0"), bank("z1")]
        y = [bank("y0"), bank("y1")]
        gate_in = [bank("gate_in0"), bank("gate_in1")]
        bulk = bank("bulk")
        mem_h = bank("mem_h")
        logits = bulk[:, 0:TOK * EXPERTS]

        def part(name):
            a, b = SMALL[name]
            return small[:, a:b]

        cond, b1, b2, ident, ones = part("cond"), part("b1"), part("b2"), part("ident"), part("ones")
        bx, bh, rec_w = part("bx"), part("bh"), part("rec")
        expert_gate = {L0: part("gate"), L1: part("router")}
        lower = part("lower").rearrange("p (e j) -> p e j", e=EXPERTS)

        def steps_of(t):
            return t.rearrange("p (s b) -> p s b", b=BATCH)

        def gates_of(b):
            return gate_in[b][:, :].rearrange("p (s c) -> p s c", c=2 * BATCH)

        small_in, x_in = sem("small_in"), sem("x_in")
        stage_in = [sem(f"stage_in{i}") for i in range(STAGE)]
        w_hi, w_lo = sem("w_hi"), sem("w_lo")
        init_act, init_dve = sem("init_act"), sem("init_dve")
        xp_ready = sem("xp_ready")
        prod_done, wdot_done, w_shifted, w_exp = sem("prod_done"), sem("wdot_done"), sem("w_shifted"), sem("w_exp")
        w_chain, v_scaled, v_done, v_hi, v_ready = sem("w_chain"), sem("v_scaled"), sem("v_done"), sem("v_hi"), sem("v_ready")
        logits_done, shifted, exp_done = per_layer("logits_done"), per_layer("shifted"), per_layer("exp_done")
        mask_chain_a, mask_chain_b = per_layer("mask_chain_a"), per_layer("mask_chain_b")
        mask_done, turned, evacuated = per_layer("mask_done"), per_layer("turned"), per_layer("evacuated")
        mask_stored = per_layer("mask_stored")
        mask_in = [sem(f"mask_in{i}") for i in range(MASKS)]
        z_done, relu_done, hi_done, y_done = (per_layer(s) for s in ("z_done", "relu_done", "hi_done", "y_done"))
        squared = sem("squared")
        lo_done = {(q, p): sem(f"lo_done{q}{'pool' if p else 'dve'}") for q in (L0, L1) for p in (False, True)}
        combined, summed = per_layer("combined"), per_layer("summed")
        x1_hi, x1_ready, xp_done, xw_done = sem("x1_hi"), sem("x1_ready"), sem("xp_done"), sem("xw_done")
        out1_begun, out_stored = sem("out1_begun"), sem("out_stored")
        hs_hi_done, hs_ready = sem("hs_hi_done"), sem("hs_ready")
        gates_in, mem_in, gates_out, half_done = sem("gates_in"), sem("mem_in"), sem("gates_out"), sem("half_done")
        reset_done, memory_done, blend_done, th_done, fresh_done = (
            sem(s) for s in ("reset_done", "memory_done", "blend_done", "th_done", "fresh_done"))
        h_done = sem("h_done")

        block = ctx.enter_context(nc.Block())

        def wait_lo(engine, t):
            engine.wait_ge(lo_done[t[0], lo_on_pool(t[0], t[1])], lo_count(t))

        def y_bank(q, e):
            return (e + q + 1) % 2

        def group_before(it, q, e, back):
            if e >= back:
                return q, it.block[q] * GROUPS[q] + (e - back + 1)
            if q == L0 and it.l1:
                return L1, it.block[L1] * GROUPS[L1] + (GROUPS[L1] + e - back + 1)
            if it.before is None:
                return None
            if it.before == L0:
                return L0, it.k * GROUPS[L0] + (GROUPS[L0] + e - back + 1)
            return L1, (it.k - 2) * GROUPS[L1] + (GROUPS[L1] + e - back + 1)

        def bank_before(it, q, e):
            for back in (1, 2):
                inside = e >= back
                pq, pe = (q, e - back) if inside else \
                    (L1, GROUPS[L1] + e - back) if (q == L0 and it.l1) else (it.before, None)
                if pq is None:
                    return None
                if pe is None:
                    pe = GROUPS[pq] + e - back
                if y_bank(pq, pe) == y_bank(q, e):
                    return group_before(it, q, e, back)

        def term_before(it, q, e):
            if e >= 2:
                return q, it.block[q] * EXPERTS + (e - 1)
            if q == L0 and it.l1:
                return L1, it.block[L1] * EXPERTS + (EXPERTS + e - 1)
            if it.before is None:
                return None
            return it.before, (it.k if it.before == L0 else it.k - 2) * EXPERTS + (EXPERTS + e - 1)

        def masks_loaded(it, q, m, carried):
            if carried:
                sets = it.k + (it.k - 1)
            elif q == L1:
                sets = it.block[L1] + (it.k + 1 if it.rec else BLOCKS)
            else:
                sets = it.block[L0] + (it.k if it.l1 else 0)
            return 16 * (sets * (EXPERTS // MASKS) + (m // MASKS + 1))

        def mask_before(it, q, m):
            if m >= MASKS:
                return q, it.block[q] * GROUPS[q] + (m - MASKS + q + 1)
            back = EXPERTS + m - MASKS + 1
            if q == L0 and it.l1:
                return L1, it.block[L1] * GROUPS[L1] + (back + 1)
            if it.before is None:
                return None
            if it.before == L0:
                return L0, it.k * GROUPS[L0] + back
            return L1, (it.k - 2) * GROUPS[L1] + (back + 1)

        @block.sync
        def _(sp):
            def load_weight(c):
                if c >= STAGE:
                    sp.wait_ge(w_lo, c - STAGE + 1)
                sp.dma_start(stage[:, c % STAGE, :], weights_dram[c]).then_inc(stage_in[c % STAGE], 16)

            def held(value):
                return value if isinstance(value, int) else sp.snap(value)

            def store_mask(q):
                def go(it):
                    sp.wait_ge(evacuated[q], it.block[q] + 1)
                    sp.dma_start(mask_dram[q], mask_t).then_inc(mask_stored[q], 16)
                return go

            def load_mask(q, m):
                def go(it):
                    prev = mask_before(it, q, m)
                    if m == 0:
                        sp.wait_ge(mask_stored[q], 16 * (it.block[q] + 1))
                        if it.l1:
                            prev = None
                    if q == L1 and m == EXPERTS - 1 and it.l0:
                        prev = mask_before(it, L0, 0)
                    if prev:
                        sp.wait_ge(combined[prev[0]], prev[1])
                    row = mask_dram[q][m:m + 1, :].to_broadcast([D, N])
                    sp.dma_start(mask_all[:, m % MASKS, :], row).then_inc(mask_in[m % MASKS], 16)
                return go

            def masks(it, q, first, last):
                for m in range(first, last):
                    load_mask(q, m)(it)

            def body(it):
                if it.l0:
                    x_at = held((it.k + 1) * N)
                if it.l1:
                    out_at = held((it.k - 1) * N)
                if it.l0:
                    if not it.rec:
                        sp.dma_start(small[:, :], small_dram).then_inc(small_in, 16)
                        sp.dma_start(xp_raw, xp_dram).then_inc(small_in, 16)
                        sp.dma_start(bias_raw, bias_dram).then_inc(small_in, 16)
                    else:
                        sp.wait_ge(summed[L0], it.k * EXPERTS + 1)
                    sp.dma_start(x_t[:, :], x_dram[:, bass.ds(x_at, N)]).then_inc(x_in, 16)
                ws = sorted(c for cs in w_slots(it).values() for c in cs)
                for c in ws[:STAGE]:
                    load_weight(c)
                if it.l1:
                    store_mask(L1)(it)
                    masks(it, L1, 0, 5)
                if it.l0:
                    store_mask(L0)(it)
                if it.l1:
                    masks(it, L1, 5, EXPERTS)
                if it.l0 and it.l1:
                    masks(it, L0, 0, 2)
                elif it.l0:
                    masks(it, L0, 0, MASKS)
                    for c in ws[STAGE:]:
                        load_weight(c)
                    masks(it, L0, MASKS, EXPERTS)
                if it.l1:
                    sp.wait_ge(summed[L1], it.k * EXPERTS)
                    sp.dma_start(out_dram[:, bass.ds(out_at, N)], out1[:, :]).then_inc(out_stored, 16)
                if it.l0 and it.l1:
                    masks(it, L0, 2, EXPERTS)

            run_passes(sp, body)
            for q in (L0, L1):
                sp.wait_ge(mask_stored[q], 16 * BLOCKS)
            sp.wait_ge(out_stored, 16 * BLOCKS)

        @block.tensor
        def _(pe):
            def product(out, w_h, w_l, x_h, x_l, start, stop):
                pe.matmul(out, w_h, x_h, start=start, stop=False)
                pe.matmul(out, w_l, x_h, start=False, stop=False)
                return pe.matmul(out, w_h, x_l, start=False, stop=stop)

            def expert_logits(q, tokens, block):
                for t in range(TOK):
                    mm = pe.matmul(logits[:, EXPERTS * t:EXPERTS * (t + 1)], tokens[:, D * t:D * (t + 1)],
                                   expert_gate[q], start=True, stop=True)
                mm.then_inc(logits_done[q], 1)

            def turn_mask(q, block):
                pe.wait_ge(mask_done[q], block + 1)
                for t in range(TOK):
                    mm = pe.transpose(bulk[0:EXPERTS, D * t:D * (t + 1)], mask[q][:, t, :], ident)
                mm.then_inc(turned[q], 1)

            def body(it):
                k = it.k
                b0, b1_ = it.block[L0], it.block[L1]
                for i in range(it.slots):
                    if it.l1 and i == it.logits1:
                        pe.wait_ge(h_done, k * STEPS)
                        if it.before == L0:
                            pe.wait_ge(evacuated[L0], k + 1)
                        else:
                            pe.wait_ge(xw_done, BLOCKS)
                        expert_logits(L1, hs, b1_)
                    if it.l1 and i == it.turn1:
                        turn_mask(L1, b1_)
                    if it.rec and i == it.xproj:
                        pe.wait_ge(x1_ready, k + 1)
                        if not it.l1:
                            pe.wait_ge(xp_ready, 1)
                        for h in range(2):
                            if it.l1:
                                pe.wait_ge(gates_out, k * STEPS - HALF * (1 - h))
                            gin = gates_of(h)
                            cols = slice(h * N // 2, (h + 1) * N // 2)
                            for c in range(2):
                                pe.matmul(gin[:, :, BATCH * c:BATCH * (c + 1)], bias_pair[:, D * c:D * (c + 1)],
                                          ones_pair[:, :].unsqueeze(1).to_broadcast([2, HALF, BATCH]),
                                          start=(c == 0), stop=False)
                            for c in range(2):
                                product(gin[:, :, BATCH * c:BATCH * (c + 1)], xp_hi[:, D * c:D * (c + 1)],
                                        xp_lo[:, D * c:D * (c + 1)], in0_hi[:, cols], in0_lo[:, cols], False, c == 1)
                        if it.l1:
                            pe.wait_ge(evacuated[L1], k)
                        else:
                            pe.wait_ge(evacuated[L0], k + 1)
                        product(bulk[:, :], xp_hi[:, 2 * D:], xp_lo[:, 2 * D:], in0_hi[:, :], in0_lo[:, :],
                                True, True).then_inc(xp_done, 1)
                    if it.l0 and i == it.wdot:
                        if it.rec:
                            pe.wait_ge(xw_done, k + 1)
                        pe.wait_ge(prod_done, b0 + 1)
                        pe.matmul(bulk[:, :], ones, v[:, :], start=True, stop=True).then_inc(wdot_done, 1)
                    if it.l0 and i == it.gates:
                        pe.wait_ge(v_done, b0 + 1)
                        expert_logits(L0, v, b0)
                    if it.l0 and i == it.turn0:
                        pe.wait_ge(w_shifted, b0 + 1)
                        turn_mask(L0, b0)
                    if i < it.n:
                        q, j, b = it.tile(i)
                        e, c = divmod(j, CHUNKS)
                        if j == 0:
                            pe.wait_ge(v_ready if q == L0 else hs_ready, b + 1)
                        if c == 0 and not it.rec and it.l0:
                            pe.wait_ge(w_lo, 2 * e + 1)
                        if it.any_tile(i - 2):
                            p = it.any_tile(i - 2)
                            pe.wait_ge(relu_done[p[0]], tile_count(p))
                        x_h, x_l = (in0_hi, in0_lo) if q == L0 else (hs_hi, hs_lo)
                        product(z[i % 2][:, :], first_hi[q][:, e, D * c:D * (c + 1)], first_lo[q][:, e, D * c:D * (c + 1)],
                                x_h[:, :], x_l[:, :], True, True).then_inc(z_done[q], 1)
                    if it.tile(i - LAG):
                        t = it.tile(i - LAG)
                        q, j, b = t
                        e, c = divmod(j, CHUNKS)
                        if c == 0 and not it.rec and it.l0:
                            pe.wait_ge(w_lo, 2 * e + 2)
                        if c == 0 and i >= LAG:
                            prev = bank_before(it, q, e)
                            if prev:
                                pe.wait_ge(combined[prev[0]], prev[1])
                        if c == 0 and i < LAG:
                            pe.wait_ge(combined[q], b * GROUPS[q] + (e - 1))
                        wait_lo(pe, t)
                        product(y[y_bank(q, e)][:, :], second_hi[q][:, e, D * c:D * (c + 1)],
                                second_lo[q][:, e, D * c:D * (c + 1)], hid_hi[:, (i - LAG) % RING, :],
                                hid_lo[:, (i - LAG) % RING, :], c == 0, c == CHUNKS - 1).then_inc(y_done[q], 1)
                    if i in it.step_at:
                        u = it.step_at[i]
                        if it.l1 or u:
                            pe.wait_ge(h_done, k * STEPS + u)
                        else:
                            pe.wait_ge(init_dve, 1)
                        h_prev = hs[:, BATCH * ((u - 1) % STEPS):BATCH * ((u - 1) % STEPS + 1)]
                        for c in range(2):
                            mm = pe.matmul(gates_of(u // HALF)[:, u % HALF, BATCH * c:BATCH * (c + 1)],
                                           rec_w[:, D * c:D * (c + 1)], h_prev, start=False, stop=True,
                                           skip_group_check=True)
                        mm.then_inc(gates_in, 1)
                        pe.matmul(mem_h[:, 0:BATCH], rec_w[:, 2 * D:], h_prev, start=True, stop=True).then_inc(mem_in, 1)
                if it.rec and not it.l1:
                    pe.wait_ge(w_lo, W_ALL)

            run_passes(pe, body)

        @block.scalar
        def _(act):
            def evacuate_mask(q, block):
                act.wait_ge(turned[q], block + 1)
                act.activation(mask_t[:, :], bulk[0:EXPERTS, :], ACT.Copy).then_inc(evacuated[q], 1)

            act.wait_ge(small_in, 48)
            act.activation(xp_hi[:, :], xp_raw, ACT.Copy).then_inc(init_act, 1)
            act.activation(bias_pair[:, :], bias_raw, ACT.Copy).then_inc(init_act, 1)
            act.activation(ones_pair[:, :], ones[0:2, 0:BATCH], ACT.Copy).then_inc(init_act, 1)

            def body(it):
                k = it.k
                b0, b1_ = it.block[L0], it.block[L1]
                weights = w_slots(it)
                for i in range(it.slots):
                    if it.l1 and i == it.exp1:
                        act.wait_ge(shifted[L1], b1_ + 1)
                        act.activation(g[L1][:, :, :], g[L1][:, :, :], ACT.Exp).then_inc(exp_done[L1], 1)
                    if it.l1 and i == it.evac1:
                        if it.before == L0:
                            act.wait_ge(mask_stored[L0], 16 * (k + 1))
                        else:
                            act.wait_ge(mask_stored[L1], 16 * b1_)
                        evacuate_mask(L1, b1_)
                    if it.rec and i == it.x1_split:
                        act.wait_ge(summed[L0], (k + 1) * EXPERTS)
                        act.activation(in0_hi[:, :], x1[:, :], ACT.Copy).then_inc(x1_hi, 1)
                    if it.rec and i == it.xw:
                        act.wait_ge(xp_done, k + 1)
                        if it.l1:
                            act.wait_ge(memory_done, k * STEPS)
                        act.activation(xw[:, :], bulk[:, :], ACT.Identity, bias=bx).then_inc(xw_done, 1)
                    if it.l0 and i == it.exp_w:
                        act.wait_ge(w_shifted, b0 + 1)
                        act.activation(v[:, :], v[:, :], ACT.Exp, scale=float(D) ** -0.5).then_inc(w_exp, 1)
                    if it.l0 and i == it.v_split:
                        act.wait_ge(v_done, b0 + 1)
                        if it.rec:
                            act.wait_ge(xp_done, k + 1)
                        act.activation(in0_hi[:, :], v[:, :], ACT.Copy).then_inc(v_hi, 1)
                    if it.l0 and i == it.exp0:
                        act.wait_ge(shifted[L0], b0 + 1)
                        act.activation(g[L0][:, :, :], g[L0][:, :, :], ACT.Exp).then_inc(exp_done[L0], 1)
                    if it.l0 and i == it.evac0:
                        if it.l1:
                            act.wait_ge(mask_stored[L1], 16 * k)
                        elif it.rec:
                            act.wait_ge(mask_stored[L0], 16 * (k + 1))
                        evacuate_mask(L0, b0)
                    if it.rec and i == it.copy1:
                        if it.l1:
                            act.wait_ge(out_stored, 16 * k)
                        act.wait_ge(summed[L0], (k + 1) * EXPERTS)
                        act.activation(out1[:, :], x1[:, :], ACT.Copy).then_inc(out1_begun, 1)
                    if i - 1 in it.step_at:
                        u = it.step_at[i - 1]
                        act.wait_ge(gates_in, k * STEPS + (u + 1))
                        act.activation(th_gates[:, :], gates_of(u // HALF)[:, u % HALF, :], ACT.Tanh, scale=0.5).then_inc(gates_out, 1)
                    for c in weights.get(i, []):
                        act.wait_ge(stage_in[c % STAGE], 16 * (c // STAGE + 1))
                        q, e, hi = (L0, c // 2, (first_hi, second_hi)[c % 2]) if c < W_L0 else \
                            (L1, (c - W_L0) // 2, (first_hi, second_hi)[c % 2])
                        act.activation(hi[q][:, e, :], stage[:, c % STAGE, :], ACT.Copy).then_inc(w_hi, 1)
                    if i < it.n:
                        t = it.tile(i)
                        q, j, _ = t
                        if it.any_tile(i - RING):
                            wait_lo(act, it.any_tile(i - RING))
                        act.wait_ge(z_done[q], tile_count(t))
                        bias = {"bias": b1[:, j:j + 1]} if q == L0 else {}
                        act.activation(hid[:, i % RING, :], z[i % 2][:, :], ACT.Relu, **bias).then_inc(relu_done[q], 1)
                    if it.tile(i - 1):
                        t = it.tile(i - 1)
                        if it.any_tile(i - 1 - RING):
                            p = it.any_tile(i - 1 - RING)
                            act.wait_ge(y_done[p[0]], tile_count(p))
                        act.wait_ge(relu_done[L0] if t[0] == L0 else squared, tile_count(t))
                        act.activation(hid_hi[:, (i - 1) % RING, :], hid[:, (i - 1) % RING, :], ACT.Copy).then_inc(hi_done[t[0]], 1)
                    if i - 1 in it.step_at:
                        u = it.step_at[i - 1]
                        act.wait_ge(memory_done, k * STEPS + (u + 1))
                        act.activation(th_mem[:, :], memory[:, :], ACT.Tanh).then_inc(th_done, 1)
                    if it.rec and i == it.hs_split:
                        act.wait_ge(h_done, (k + 1) * STEPS)
                        if it.l1:
                            act.wait_ge(z_done[L1], k * TILES[L1])
                        act.activation(hs_hi[:, :], hs[:, :], ACT.Copy).then_inc(hs_hi_done, 1)

            run_passes(act, body)

        @block.vector
        def _(dve):
            w_link = Chain(dve, w_chain, 4)
            link_a = {L0: Chain(dve, mask_chain_a[L0], 3), L1: Chain(dve, mask_chain_a[L1], 1)}
            link_b = {L0: Chain(dve, mask_chain_b[L0], 3), L1: Chain(dve, mask_chain_b[L1], 11)}

            def over_experts(column):
                return column.unsqueeze(2).to_broadcast([D, TOK, EXPERTS])

            def over_steps(per_step):
                return per_step.unsqueeze(2).to_broadcast([D, STEPS, BATCH])

            dve.wait_ge(small_in, 48)
            dve.tensor_copy(hs[:, BATCH * (STEPS - 1):], cond).then_inc(init_dve, 1)
            dve.wait_ge(init_act, 3)
            dve.tensor_tensor(xp_lo[:, :], xp_raw, xp_hi[:, :], ALU.subtract).then_inc(init_dve, 1)
            dve.tensor_tensor(bias_raw, bias_raw, bias_pair[:, :], ALU.subtract).then_inc(init_dve, 1)
            pick = small[0:2, SMALL["pick"][0]:SMALL["pick"][1]]
            dve.wait_ge(init_dve, 3)
            dve.tensor_scalar(bias_raw, bias_raw, pick[:, 1:2], None, ALU.mult).then_inc(init_dve, 1)
            dve.wait_ge(init_dve, 4)
            dve.scalar_tensor_tensor(out=bias_pair[:, :], in0=bias_pair[:, :], scalar=pick[:, 0:1], in1=bias_raw,
                                     op0=ALU.mult, op1=ALU.add).then_inc(xp_ready, 1)

            def mask0_a(b):
                link = link_a[L0]
                link.begin(b)
                dve.wait_ge(logits_done[L0], b + 1)
                link(dve.tensor_copy(kept[:, :, :], logits.rearrange("p (t e) -> p t e", e=EXPERTS)))
                dve.tensor_reduce(stat[L0][:, 2, :], kept[:, :, :], AX.X, ALU.max)
                for t in range(TOK):
                    last = dve.max(top[:, t, :], kept[:, t, :])
                link(last)
                dve.tensor_tensor(g[L0][:, :, :], kept[:, :, :], over_experts(stat[L0][:, 2, :]), ALU.subtract).then_inc(shifted[L0], 1)
                link(dve.tensor_tensor(kept[:, :, :], kept[:, :, :], over_experts(top[:, :, 1]), ALU.is_ge))

            def mask0_b(b):
                link = link_b[L0]
                link.begin(b)
                s = stat[L0]
                dve.wait_ge(exp_done[L0], b + 1)
                link(dve.tensor_tensor(kept[:, :, :], g[L0][:, :, :], kept[:, :, :], ALU.mult))
                link(dve.tensor_reduce(s[:, 0, :], kept[:, :, :], AX.X, ALU.add))
                link(dve.reciprocal(s[:, 1, :], s[:, 0, :]))
                dve.scalar_tensor_tensor(out=mask[L0][:, :, :], in0=kept[:, :, :], scalar=1.0 / EXPERTS,
                                         in1=over_experts(s[:, 1, :]), op0=ALU.mult, op1=ALU.mult).then_inc(mask_done[L0], 1)

            def mask1_a(b):
                link = link_a[L1]
                link.begin(b)
                lg = logits.rearrange("p (t e) -> p t e", e=EXPERTS)
                dve.wait_ge(logits_done[L1], b + 1)
                link(dve.tensor_reduce(stat[L1][:, 0, :], lg, AX.X, ALU.max))
                dve.tensor_tensor(g[L1][:, :, :], lg, over_experts(stat[L1][:, 0, :]), ALU.subtract).then_inc(shifted[L1], 1)

            def mask1_b(b, before):
                link = link_b[L1]
                link.begin(b)
                s = stat[L1]
                dve.wait_ge(exp_done[L1], b + 1)
                link(dve.tensor_reduce(s[:, 1, :], g[L1][:, :, :], AX.X, ALU.add))
                link(dve.reciprocal(s[:, 2, :], s[:, 1, :]))
                link(dve.tensor_tensor(prob[:, :, :], g[L1][:, :, :], over_experts(s[:, 2, :]), ALU.mult))
                if before == L0:
                    dve.wait_ge(mask_stored[L0], 16 * (b + 2))
                else:
                    dve.wait_ge(mask_stored[L1], 16 * b)
                full = [D, TOK, EXPERTS, EXPERTS]
                other = prob[:, :, :].unsqueeze(2).to_broadcast(full)
                own = prob[:, :, :].unsqueeze(3).to_broadcast(full)
                dve.tensor_tensor(above, other, own, ALU.is_gt)
                link(dve.tensor_tensor(equal, other, own, ALU.is_equal))
                link(dve.tensor_tensor(equal, equal, lower.unsqueeze(1).to_broadcast(full), ALU.mult))
                link(dve.tensor_tensor(above, above, equal, ALU.add))
                link(dve.tensor_reduce(rank[:, :, :], above, AX.X, ALU.add))
                link(dve.scalar_tensor_tensor(out=prob[:, :, :], in0=rank[:, :, :], scalar=2.0, in1=prob[:, :, :],
                                              op0=ALU.is_lt, op1=ALU.mult))
                link(dve.tensor_reduce(s[:, 3, :], prob[:, :, :], AX.X, ALU.add))
                link(dve.tensor_scalar(s[:, 3, :], s[:, 3, :], 1e-9, None, ALU.max))
                link(dve.reciprocal(s[:, 3, :], s[:, 3, :]))
                dve.tensor_tensor(mask[L1][:, :, :], prob[:, :, :], over_experts(s[:, 3, :]), ALU.mult).then_inc(mask_done[L1], 1)

            def combine(it, q, e, b, carried):
                dve.wait_ge(y_done[q], b * TILES[q] + CHUNKS * (e + 1))
                out_y = y[y_bank(q, e)][:, :]
                if q == L1 and e == 0:
                    dve.wait_ge(out1_begun, b + 1)
                    dve.tensor_tensor(out1[:, :], out_y, out1[:, :], ALU.add).then_inc(combined[L1], 1)
                    return
                m = e - q
                if m >= 2:
                    dve.wait_ge(summed[q], b * EXPERTS + (m - 1))
                else:
                    prev = term_before(it, q, m)
                    if prev:
                        dve.wait_ge(summed[prev[0]], prev[1])
                dve.wait_ge(mask_in[m % MASKS], masks_loaded(it, q, m, carried))
                if q == L0:
                    ins = dve.scalar_tensor_tensor(out=term[:, m % 2, :], in0=out_y, scalar=b2[:, e:e + 1],
                                                   in1=mask_all[:, m % MASKS, :], op0=ALU.add, op1=ALU.mult)
                else:
                    ins = dve.tensor_tensor(term[:, m % 2, :], out_y, mask_all[:, m % MASKS, :], ALU.mult)
                ins.then_inc(combined[q], 1)

            def body(it):
                k = it.k
                b0, b1_ = it.block[L0], it.block[L1]
                weights = w_slots(it)
                for i in range(it.slots):
                    if it.l1 and i == it.mask1a:
                        mask1_a(b1_)
                    if it.l1 and i == it.mask1b:
                        mask1_b(b1_, it.before)
                    if it.rec and i == it.x1_split:
                        dve.wait_ge(x1_hi, k + 1)
                        dve.tensor_tensor(in0_lo[:, :], x1[:, :], in0_hi[:, :], ALU.subtract).then_inc(x1_ready, 1)
                    if it.l0 and i == it.shift:
                        w_link.begin(b0)
                        dve.wait_ge(wdot_done, b0 + 1)
                        w_link(dve.tensor_reduce(w_max[:, :], steps_of(bulk[:, :]), AX.X, ALU.max))
                        dve.tensor_tensor(steps_of(v[:, :]), steps_of(bulk[:, :]), over_steps(w_max[:, :]), ALU.subtract).then_inc(w_shifted, 1)
                    if it.l0 and i == it.scale:
                        dve.wait_ge(w_exp, b0 + 1)
                        w_link(dve.tensor_reduce(w_sum[:, :], steps_of(v[:, :]), AX.X, ALU.add))
                        w_link(dve.reciprocal(w_inv[:, :], w_sum[:, :]))
                        w_link(dve.tensor_tensor(steps_of(v[:, :]), steps_of(v[:, :]), over_steps(w_inv[:, :]), ALU.mult))
                        dve.tensor_tensor(v[:, :], v[:, :], x_t[:, :], ALU.mult).then_inc(v_done, 1)
                    if it.l0 and i == it.v_split:
                        dve.wait_ge(v_hi, b0 + 1)
                        dve.tensor_tensor(in0_lo[:, :], v[:, :], in0_hi[:, :], ALU.subtract).then_inc(v_ready, 1)
                    if it.l0 and i == it.mask0a:
                        mask0_a(b0)
                    if it.l0 and i == it.mask0b:
                        mask0_b(b0)
                    if i - 1 in it.step_at:
                        u = it.step_at[i - 1]
                        n = k * STEPS + (u + 1)
                        h_prev = hs[:, BATCH * ((u - 1) % STEPS):BATCH * ((u - 1) % STEPS + 1)]
                        dve.wait_ge(mem_in, n)
                        dve.tensor_scalar(memory[:, :], mem_h[:, 0:BATCH], bh, 0.5, ALU.add, ALU.mult).then_inc(half_done, 1)
                        dve.wait_ge(gates_out, n)
                        dve.wait_ge(half_done, n)
                        dve.scalar_tensor_tensor(out=memory[:, :], in0=th_gates[:, 0:BATCH], scalar=1.0, in1=memory[:, :],
                                                 op0=ALU.add, op1=ALU.mult).then_inc(reset_done, 1)
                        dve.wait_ge(reset_done, n)
                        if u == 0:
                            dve.wait_ge(xw_done, k + 1)
                        dve.tensor_tensor(memory[:, :], memory[:, :], xw[:, BATCH * u:BATCH * (u + 1)], ALU.add).then_inc(memory_done, 1)
                        dve.tensor_scalar(keep_not[:, :], th_gates[:, BATCH:], -0.5, 0.5, ALU.mult, ALU.add)
                        dve.scalar_tensor_tensor(out=keep2[:, :], in0=th_gates[:, BATCH:], scalar=1.0, in1=h_prev,
                                                 op0=ALU.add, op1=ALU.mult).then_inc(blend_done, 1)
                    for c in weights.get(i, []):
                        dve.wait_ge(w_hi, c + 1)
                        q, e = (L0, c // 2) if c < W_L0 else (L1, (c - W_L0) // 2)
                        hi, lo = ((first_hi, first_lo), (second_hi, second_lo))[c % 2]
                        dve.tensor_tensor(lo[q][:, e, :], stage[:, c % STAGE, :], hi[q][:, e, :], ALU.subtract).then_inc(w_lo, 1)
                    if i < it.n and it.tile(i)[0] == L1:
                        dve.wait_ge(relu_done[L1], tile_count(it.tile(i)))
                        h = hid[:, i % RING, :]
                        dve.tensor_tensor(h, h, h, ALU.mult).then_inc(squared, 1)
                    t = it.tile(i - 1)
                    if t and not lo_on_pool(*t[:2]):
                        dve.wait_ge(hi_done[t[0]], tile_count(t))
                        s = (i - 1) % RING
                        dve.tensor_tensor(hid_lo[:, s, :], hid[:, s, :], hid_hi[:, s, :], ALU.subtract).then_inc(lo_done[t[0], False], 1)
                    t = it.tile(i - 1 - LAG)
                    if t and t[1] % CHUNKS == CHUNKS - 1:
                        combine(it, t[0], t[1] // CHUNKS, t[2], i - 1 - LAG < 0)
                    if i - 1 in it.step_at:
                        u = it.step_at[i - 1]
                        n = k * STEPS + (u + 1)
                        dve.wait_ge(blend_done, n)
                        dve.wait_ge(th_done, n)
                        dve.tensor_tensor(th_mem[:, :], keep_not[:, :], th_mem[:, :], ALU.mult).then_inc(fresh_done, 1)
                        if u == 0 and it.l1:
                            dve.wait_ge(logits_done[L1], b1_ + 1)
                            dve.wait_ge(hs_ready, k)
                        dve.wait_ge(fresh_done, n)
                        dve.scalar_tensor_tensor(out=hs[:, BATCH * u:BATCH * (u + 1)], in0=keep2[:, :], scalar=0.5,
                                                 in1=th_mem[:, :], op0=ALU.mult, op1=ALU.add).then_inc(h_done, 1)
                    if it.rec and i == it.hs_split:
                        dve.wait_ge(hs_hi_done, k + 1)
                        dve.tensor_tensor(hs_lo[:, :], hs[:, :], hs_hi[:, :], ALU.subtract).then_inc(hs_ready, 1)

            run_passes(dve, body)

        @block.gpsimd
        def _(pool):
            def body(it):
                k = it.k
                b0, b1_ = it.block[L0], it.block[L1]
                for i in range(it.slots):
                    if it.l0 and i == it.prod:
                        if not it.rec:
                            pool.wait_ge(small_in, 48)
                        else:
                            pool.wait_ge(logits_done[L0], b0)
                            pool.wait_ge(v_ready, b0)
                        pool.wait_ge(x_in, 16 * (b0 + 1))
                        pool.tensor_tensor(steps_of(v[:, :]), steps_of(x_t[:, :]),
                                           cond.unsqueeze(1).to_broadcast([D, STEPS, BATCH]), ALU.mult).then_inc(prod_done, 1)
                    t = it.tile(i - 1)
                    if t and lo_on_pool(*t[:2]):
                        pool.wait_ge(hi_done[t[0]], tile_count(t))
                        s = (i - 1) % RING
                        pool.tensor_tensor(hid_lo[:, s, :], hid[:, s, :], hid_hi[:, s, :], ALU.subtract).then_inc(lo_done[t[0], True], 1)
                    t = it.tile(i - 2 - LAG)
                    if t and t[1] % CHUNKS == CHUNKS - 1 and not (t[0] == L1 and t[1] < CHUNKS):
                        q, j, b = t
                        e = j // CHUNKS
                        m = e - q
                        pool.wait_ge(combined[q], b * GROUPS[q] + (e + 1))
                        if q == L0 and m == 0:
                            if it.rec:
                                pool.wait_ge(out1_begun, k + 1)
                                pool.wait_ge(x1_ready, k + 1)
                            pool.tensor_tensor(x1[:, :], term[:, 0, :], x_t[:, :], ALU.add).then_inc(summed[L0], 1)
                        else:
                            acc = x1 if q == L0 else out1
                            if m:
                                pool.wait_ge(summed[q], b * EXPERTS + m)
                            pool.tensor_tensor(acc[:, :], term[:, m % 2, :], acc[:, :], ALU.add).then_inc(summed[q], 1)

            run_passes(pool, body)


def kernel(**inputs):
    import numpy as np
    import concourse.bacc as bacc
    from concourse.bass_utils import run_bass_kernel_spmd

    a = {n: np.asarray(v) for n, v in inputs.items()}
    x_t = np.ascontiguousarray(a["x"].transpose(2, 1, 0)).reshape(D, SEQ * BATCH)

    def second(w):
        return w.reshape(CHUNKS, D, D).transpose(1, 0, 2).reshape(D, N)

    pieces = []
    for e in range(EXPERTS):
        pieces += [a["L0_ffn_W1"][e], second(a["L0_ffn_W2"][e])]
    pieces += [a["L1_ffn_shared_fc"].T, second(a["L1_ffn_shared_proj"].T)]
    for e in range(EXPERTS):
        pieces += [a["L1_ffn_w_fc"][e].T, second(a["L1_ffn_w_proj"][e].T)]
    weights = np.ascontiguousarray(np.stack(pieces))

    small = np.zeros((D, SMALL_COLS), np.float32)

    def put(name, value, rows=D):
        lo, hi = SMALL[name]
        small[0:rows, lo:hi] = value

    put("cond", a["cond_1024"].T)
    put("b1", a["L0_ffn_b1"].reshape(EXPERTS * CHUNKS, D).T)
    put("b2", a["L0_ffn_b2"].T)
    put("bx", a["L1_cond_wx_b"].reshape(D, 1))
    put("bh", a["L1_cond_wh_b"].reshape(D, 1))
    put("gate", a["L0_ffn_W_gate"])
    put("router", a["L1_ffn_router_w"].T)
    put("rec", np.concatenate([a["L1_cond_w_W"][D:], a["L1_cond_wh_W"]], axis=1))
    put("ident", np.eye(D, dtype=np.float32))
    put("ones", 1.0)
    put("lower", np.tril(np.ones((EXPERTS, EXPERTS), np.float32), -1).reshape(1, -1))
    put("pick", np.eye(2, dtype=np.float32), rows=2)

    nc = bacc.Bacc("TRN2", target_bir_lowering=False, num_devices=1)
    arrays = {"x_in": x_t, "weights_in": weights, "small_in": small,
              "xp_in": np.concatenate([a["L1_cond_w_W"][:D], a["L1_cond_wx_W"]], axis=1),
              "gate_bias_in": np.stack([a["L1_cond_w_b"]] * 2)}
    ins = [nc.dram_tensor(n, v.shape, F32, kind="ExternalInput").ap() for n, v in arrays.items()]
    out = nc.dram_tensor("out_t", (D, SEQ * BATCH), F32, kind="ExternalOutput").ap()
    mask_dram = {q: nc.dram_tensor(f"mask_scratch{q}", (EXPERTS, N), F32, kind="Internal").ap() for q in (L0, L1)}
    build(nc, *ins, mask_dram, out)
    r = run_bass_kernel_spmd(nc, [arrays], core_ids=[0])
    got = np.asarray(r.results[0]["out_t"]).reshape(D, SEQ, BATCH)
    return np.ascontiguousarray(got.transpose(2, 1, 0))
```

```python
from contextlib import ExitStack

import concourse.bass as bass
from concourse import mybir

F32 = mybir.dt.float32
F32R = mybir.dt.float32r
ALU = mybir.AluOpType
ACT = mybir.ActivationFunctionType
AX = mybir.AxisListType

D = 128
SEQ = 128
BATCH = 32
STEPS = 16
N = STEPS * BATCH
BLOCKS = SEQ // STEPS
EXPERTS = 8
CHUNKS = 4
HALF = STEPS // 2
TOK = N // D
LAG = 4
RING = 4
L0, L1 = 0, 1
GROUPS = {L0: EXPERTS, L1: EXPERTS + 1}
TILES = {q: GROUPS[q] * CHUNKS for q in (L0, L1)}
STAGE = 2
MASKS = 4
W_L0 = 2 * GROUPS[L0]
W_ALL = 2 * (GROUPS[L0] + GROUPS[L1])

PLAN = {
    "first": {
        "prod": (0, 22), "wdot": (0, 27), "softmax": ([0, 0, 0, 0, 0], [28, 29, 32, 33, 34]), "exp_w": (0, 29),
        "v_mult": (4, 34), "v_split": (0,), "gates": (1, 38),
        "mask0": ([1, 1, 1, 2, 2, 2, 2], [39, 41, 43, 46, 47, 48, 49]), "exp0": (2, 45), "turn0": (3, 55),
        "evac0": (4, 56), "x_load": (0, 20), "store0": (5, 53), "load0": ([6, 6, 6, 6, 18, 26, 34, 42],),
        "prepare_rec": (3,),
    },
    "second": {
        "v_split": 0, "x1_split": 12, "copy1": 13, "xproj": 16, "xw": 17, "load0": [0, 0, 1, 9, 17, 25, 33, 41],
        "rec": (17, 3.0, 0, 0, 1, 1),
    },
    "full": {
        "logits1": 0, "exp1": 8, "mask1": [2, 3, 8, 9, 10, 11, 12, 13, 14, 16, 16, 17, 18, 19, 20], "turn1": 22,
        "evac1": 22, "x1_split": 13, "xproj": 20, "xw": 21, "prod": 20, "wdot": 28, "softmax": [29, 31, 34, 35, 36],
        "exp_w": 34, "v_mult": 38, "v_split": 44, "gates": 48, "mask0": [47, 48, 49, 56, 57, 58, 59], "exp0": 52,
        "turn0": 62, "evac0": 65, "copy1": 90, "x_load": 3, "store1": 25, "load1": [26, 26, 26, 26, 27, 33, 41, 57],
        "store0": 65, "load0": [66, 67, 73, 81, 89, 97, 105, 113], "out_store": 88, "rec": (22, 7.1, 0, 0, 2, 2),
    },
    "seventh": {
        "logits1": 0, "exp1": 4, "mask1": [0, 0, 2, 3, 4, 5, 6, 7, 8, 9, 10, 11, 12, 13, 14], "turn1": 22,
        "evac1": 22, "x1_split": 12, "xproj": 19, "xw": 18, "store1": 25, "load1": [26, 26, 26, 26, 27, 33, 41, 49],
        "out_store": 83, "rec": (20, 3.0, 0, 0, 1, 1),
    },
    "last": {
        "logits1": 0, "exp1": 5, "mask1": [1, 2, 5, 6, 7, 8, 9, 10, 11, 12, 13, 14, 15, 16, 16], "turn1": 23,
        "evac1": 19, "copy1": 9, "store1": 25, "load1": [26, 26, 26, 26, 27, 33, 41, 49], "out_store": 83,
    },
}

SMALL = {}
_at = 0
for _name, _width in (("cond", BATCH), ("ones", D), ("b1", EXPERTS * CHUNKS), ("b2", EXPERTS), ("bx", 1), ("bh", 1),
                      ("gate", EXPERTS), ("router", EXPERTS), ("rec", 3 * D), ("ident", D),
                      ("lower", EXPERTS * EXPERTS), ("pick", 2)):
    SMALL[_name] = (_at, _at + _width)
    _at += _width
SMALL_COLS = _at
SMALL_FIRST = BATCH + D


def lo_on_pool(q, j):
    return j % 2 == 1


class Pass:

    def __init__(self, k, plan, l1, rec, l0, flush, before):
        self.k, self.l1, self.rec, self.l0 = k, l1, rec, l0
        self.flush = flush
        self.before = before
        self.carry = before is not None and plan != "last"
        self.block = {L0: k + 1, L1: k - 1}
        self.tiles = [(L1, j) for j in range(TILES[L1] if l1 else 0)] + [(L0, j) for j in range(TILES[L0] if l0 else 0)]
        self.n = len(self.tiles)
        self.at = {}
        own = {"logits1": k - 1, "exp1": k - 1, "mask1": k - 1, "turn1": k - 1, "evac1": k - 1,
               "store1": k - 1, "load1": k - 1, "out_store": k - 1,
               "x1_split": k, "xproj": k, "xw": k, "copy1": k - 1 if plan == "last" else k}
        for name, places in PLAN[plan].items():
            if name == "rec":
                continue
            blocks = (0, 1) if plan == "first" else (own.get(name, k + 1),)
            for place, block in zip(places if plan == "first" else (places,), blocks):
                for stage, h in enumerate(place if isinstance(place, list) else [place]):
                    self.at.setdefault((name, h), []).append((stage, block))
        self.step_of = {}
        last = 0
        if rec:
            start, stride, *later = PLAN[plan]["rec"]
            for u in range(STEPS):
                for part, d in zip(("hidden", "sigmoid", "memory", "tanh", "state"), [0] + later):
                    h = int(start + u * stride) + d
                    self.step_of.setdefault((part, h), []).append(u)
                    last = max(last, h)
        self.hs_split = last + 1
        if not flush and self.l1:
            self.hs_split = min(last + 1, 2 * self.n - 1)
        self.slots = max(self.n + (LAG + 3 if flush else 0), self.hs_split // 2 + 1 if rec else 0)

    def stage(self, name, h):
        return self.at.get((name, h), [])

    def steps(self, part, h):
        return self.step_of.get((part, h), [])

    def works(self, i):
        return i < self.n or self.flush

    def tile(self, i):
        if i >= self.n or (i < 0 and not self.carry):
            return None
        return self.any_tile(i)

    def any_tile(self, i):
        if i >= 0:
            q, j = self.tiles[i]
            return q, j, self.block[q]
        if self.before is None:
            return None
        return self.before, TILES[self.before] + i, (self.k if self.before == L0 else self.k - 2)


def first_passes():
    return [Pass(-1, "first", False, False, True, False, None), Pass(0, "second", False, True, True, False, L0)]


def loop_pass(k):
    return Pass(k, "full", True, True, True, False, L0)


def last_passes():
    return [Pass(BLOCKS - 1, "seventh", True, True, False, True, L0), Pass(BLOCKS, "last", True, False, False, True, L1)]


def run_passes(engine, body):
    for it in first_passes():
        body(it)
    with engine.Fori(1, BLOCKS - 1) as k:
        body(loop_pass(k))
    for it in last_passes():
        body(it)


def tile_count(t):
    q, j, block = t
    return block * TILES[q] + (j + 1)


def lo_count(t):
    q, j, block = t
    mine = lo_on_pool(q, j)
    per = sum(lo_on_pool(q, i) == mine for i in range(TILES[q]))
    return block * per + sum(lo_on_pool(q, i) == mine for i in range(j + 1))


def w_slots(it):
    out = {}
    if it.l0 and not it.rec:
        for c in range(W_L0):
            out.setdefault(0 if c < 2 else CHUNKS * (c // 2 - 1) + 2 * (c % 2), []).append(c)
    elif it.l0 and not it.l1:
        for c in range(W_L0, W_ALL):
            out.setdefault(1 + (c - W_L0) * (TILES[L0] - 4) // (W_ALL - W_L0), []).append(c)
    return out


def w_loads(it):
    slot = {c: i for i, cs in w_slots(it).items() for c in cs}
    out = {}
    for c in sorted(slot):
        out.setdefault(2 * slot[c - STAGE] + 1 if c - STAGE in slot else 0, []).append(c)
    return out


class Chain:

    def __init__(self, engine, sem, steps):
        self.engine, self.sem, self.steps = engine, sem, steps

    def begin(self, block):
        self.base, self.n = block * self.steps, 0

    def __call__(self, instruction):
        self.n += 1
        assert self.n <= self.steps
        instruction.then_inc(self.sem, 1)

    def ready(self):
        self.engine.wait_ge(self.sem, self.base + self.n)


def build(nc, x_dram, weights_dram, small_dram, xp_dram, bias_dram, mask_dram, out_dram):
    with ExitStack() as ctx:
        def sb(name, shape, dt=F32):
            return ctx.enter_context(nc.sbuf_tensor(name, shape, dt))

        def bank(name):
            return ctx.enter_context(nc.psum_tensor(name, [D, N], F32))

        def sem(name):
            return ctx.enter_context(nc.semaphore(name))

        def per_layer(name):
            return {q: sem(f"{name}{q}") for q in (L0, L1)}

        first_hi = {q: sb(f"first_hi{q}", [D, GROUPS[q], N], F32R) for q in (L0, L1)}
        first_lo = {q: sb(f"first_lo{q}", [D, GROUPS[q], N], F32R) for q in (L0, L1)}
        second_hi = {q: sb(f"second_hi{q}", [D, GROUPS[q], N], F32R) for q in (L0, L1)}
        second_lo = {q: sb(f"second_lo{q}", [D, GROUPS[q], N], F32R) for q in (L0, L1)}
        small = sb("small", [D, SMALL_COLS])
        xp_hi = sb("xp_hi", [D, 3 * D], F32R)
        xp_lo = sb("xp_lo", [D, 3 * D], F32R)
        bias_pair = sb("bias_pair", [2, 2 * D], F32R)
        ones_pair = sb("ones_pair", [2, BATCH], F32R)

        x_t = sb("x_t", [D, N])
        v = sb("v", [D, N])
        in0_hi = sb("in0_hi", [D, N], F32R)
        in0_lo = sb("in0_lo", [D, N], F32R)
        x1 = sb("x1", [D, N])
        hs = sb("hs", [D, N])
        hs_hi = sb("hs_hi", [D, N], F32R)
        hs_lo = sb("hs_lo", [D, N], F32R)
        xw = sb("xw", [D, N])
        out1 = sb("out1", [D, N])
        hid = sb("hid", [D, RING, N])
        hid_hi = sb("hid_hi", [D, RING, N], F32R)
        hid_lo = sb("hid_lo", [D, RING, N], F32R)
        term = sb("term", [D, 2, N])
        mask_all = sb("mask_all", [D, MASKS, N])
        compare = sb("compare", [D, N])
        mask_t = compare[0:EXPERTS, :]

        stage = sb("stage", [D, STAGE, N])
        xp_raw = xw[:, 0:3 * D]
        bias_raw = hs[0:2, 0:2 * D]

        w_max = sb("w_max", [D, STEPS])
        w_sum = sb("w_sum", [D, STEPS])
        w_inv = sb("w_inv", [D, STEPS])
        g = {q: sb(f"g{q}", [D, TOK, EXPERTS]) for q in (L0, L1)}
        top = sb("top", [D, TOK, 8])
        kept = sb("kept", [D, TOK, EXPERTS])
        stat = {q: sb(f"stat{q}", [D, 4, TOK]) for q in (L0, L1)}
        mask = {q: sb(f"mask{q}", [D, TOK, EXPERTS]) for q in (L0, L1)}
        prob = sb("prob", [D, TOK, EXPERTS])
        rank = sb("rank", [D, TOK, EXPERTS])
        above, equal = (compare[:, N // 2 * a:N // 2 * (a + 1)].rearrange("p (t e j) -> p t e j", t=TOK, e=EXPERTS) for a in range(2))
        th_gates = sb("th_gates", [D, 2 * BATCH])
        memory = sb("memory", [D, BATCH])
        th_mem = sb("th_mem", [D, BATCH])
        keep_not = sb("keep_not", [D, BATCH])
        keep2 = sb("keep2", [D, BATCH])

        z = [bank("z0"), bank("z1")]
        y = [bank("y0"), bank("y1")]
        gate_in = [bank("gate_in0"), bank("gate_in1")]
        bulk = bank("bulk")
        mem_h = bank("mem_h")
        logits = bulk[:, 0:TOK * EXPERTS]

        def part(name):
            a, b = SMALL[name]
            return small[:, a:b]

        cond, b1, b2, ident, ones = part("cond"), part("b1"), part("b2"), part("ident"), part("ones")
        bx, bh, rec_w = part("bx"), part("bh"), part("rec")
        expert_gate = {L0: part("gate"), L1: part("router")}
        lower = part("lower").rearrange("p (e j) -> p e j", e=EXPERTS)

        def steps_of(t):
            return t.rearrange("p (s b) -> p s b", b=BATCH)

        def gates_of(b):
            return gate_in[b][:, :].rearrange("p (s c) -> p s c", c=2 * BATCH)

        cond_in, small_in, x_in = sem("cond_in"), sem("small_in"), sem("x_in")
        stage_in = [sem(f"stage_in{i}") for i in range(STAGE)]
        w_hi, w_lo = sem("w_hi"), sem("w_lo")
        init_act, init_dve = sem("init_act"), sem("init_dve")
        xp_ready = sem("xp_ready")
        prod_done, wdot_done, w_shifted, w_exp = sem("prod_done"), sem("wdot_done"), sem("w_shifted"), sem("w_exp")
        w_chain, v_scaled, v_done, v_hi, v_ready = sem("w_chain"), sem("v_scaled"), sem("v_done"), sem("v_hi"), sem("v_ready")
        logits_done, shifted, exp_done = per_layer("logits_done"), per_layer("shifted"), per_layer("exp_done")
        mask_chain_a, mask_chain_b = per_layer("mask_chain_a"), per_layer("mask_chain_b")
        mask_done, turned, evacuated = per_layer("mask_done"), per_layer("turned"), per_layer("evacuated")
        mask_stored = per_layer("mask_stored")
        mask_in = [sem(f"mask_in{i}") for i in range(MASKS)]
        z_done, relu_done, hi_done, y_done = (per_layer(s) for s in ("z_done", "relu_done", "hi_done", "y_done"))
        squared = sem("squared")
        lo_done = {(q, p): sem(f"lo_done{q}{'pool' if p else 'dve'}") for q in (L0, L1) for p in (False, True)}
        combined, summed = per_layer("combined"), per_layer("summed")
        x1_hi, x1_ready, xp_done, xw_done = sem("x1_hi"), sem("x1_ready"), sem("xp_done"), sem("xw_done")
        out1_begun, out_stored = sem("out1_begun"), sem("out_stored")
        hs_hi_done, hs_ready = sem("hs_hi_done"), sem("hs_ready")
        gates_in, mem_in, gates_out, half_done = sem("gates_in"), sem("mem_in"), sem("gates_out"), sem("half_done")
        reset_done, memory_done, blend_done, th_done, fresh_done = (
            sem(s) for s in ("reset_done", "memory_done", "blend_done", "th_done", "fresh_done"))
        h_done = sem("h_done")

        block = ctx.enter_context(nc.Block())

        def wait_lo(engine, t):
            engine.wait_ge(lo_done[t[0], lo_on_pool(t[0], t[1])], lo_count(t))

        def y_bank(q, e):
            return bulk if q == L1 and e == 0 else y[(e - q) % 2]

        def output_before(it, q, m):
            if m >= 2:
                return q, it.block[q] * GROUPS[q] + (m - 2 + q + 1)
            if q == L0 and it.l1:
                return L1, it.block[L1] * GROUPS[L1] + (GROUPS[L1] + m - 1)
            if it.before is None:
                return None
            return it.before, (it.k if it.before == L0 else it.k - 2) * GROUPS[it.before] + (GROUPS[it.before] + m - 1)

        def term_before(it, q, e):
            if e >= 2:
                return q, it.block[q] * EXPERTS + (e - 1)
            if q == L0 and it.l1:
                return L1, it.block[L1] * EXPERTS + (EXPERTS + e - 1)
            if it.before is None:
                return None
            return it.before, (it.k if it.before == L0 else it.k - 2) * EXPERTS + (EXPERTS + e - 1)

        def masks_loaded(it, q, m, carried):
            if carried:
                sets = it.k + (it.k - 1) if it.l1 else it.k
            elif q == L1:
                sets = it.block[L1] + (it.k + 1 if it.rec else BLOCKS)
            else:
                sets = it.block[L0] + (it.k if it.l1 else 0)
            return 16 * (sets * (EXPERTS // MASKS) + (m // MASKS + 1))

        def mask_before(it, q, m):
            if m >= MASKS:
                return q, it.block[q] * GROUPS[q] + (m - MASKS + q + 1)
            back = EXPERTS + m - MASKS + 1
            if q == L0 and it.l1:
                return L1, it.block[L1] * GROUPS[L1] + (back + 1)
            if it.before is None:
                return None
            if it.before == L0:
                return L0, it.k * GROUPS[L0] + back
            return L1, (it.k - 2) * GROUPS[L1] + (back + 1)

        @block.sync
        def _(sp):
            def load_weight(c):
                if c >= STAGE:
                    sp.wait_ge(w_lo, c - STAGE + 1)
                sp.dma_start(stage[:, c % STAGE, :], weights_dram[c]).then_inc(stage_in[c % STAGE], 16)

            def held(value):
                return value if isinstance(value, int) else sp.snap(value)

            def store_mask(q, b):
                if isinstance(b, int) and (q, b) == (L0, 1):
                    for sem_in in mask_in:
                        sp.wait_ge(sem_in, 16 * (EXPERTS // MASKS))
                sp.wait_ge(evacuated[q], b + 1)
                sp.dma_start(mask_dram[q], mask_t).then_inc(mask_stored[q], 16)

            def load_mask(it, q, m, b):
                prev = mask_before(it, q, m)
                if m == 0:
                    sp.wait_ge(mask_stored[q], 16 * (b + 1))
                    if it.l1:
                        prev = None
                if q == L1 and m == EXPERTS - 1 and it.l0:
                    prev = mask_before(it, L0, 0)
                if prev:
                    sp.wait_ge(combined[prev[0]], prev[1])
                row = mask_dram[q][m:m + 1, :].to_broadcast([D, N])
                sp.dma_start(mask_all[:, m % MASKS, :], row).then_inc(mask_in[m % MASKS], 16)

            def body(it):
                if it.l0:
                    x_at = held((it.k + 1) * N)
                if it.l1:
                    out_at = held((it.k - 1) * N)
                loads = w_loads(it)
                for h in range(2 * it.slots):
                    for _, b in it.stage("x_load", h):
                        if it.l1:
                            sp.wait_ge(summed[L0], it.k * EXPERTS + 1)
                            sp.dma_start(x_t[:, :], x_dram[:, bass.ds(x_at, N)]).then_inc(x_in, 16)
                        elif b:
                            sp.wait_ge(summed[L0], 1)
                            sp.dma_start(x_t[:, :], x_dram[:, bass.ds(N, N)]).then_inc(x_in, 16)
                        else:
                            sp.dma_start(small[:, 0:SMALL_FIRST], small_dram[:, 0:SMALL_FIRST]).then_inc(cond_in, 16)
                            sp.dma_start(x_t[:, :], x_dram[:, 0:N]).then_inc(x_in, 16)
                            sp.dma_start(small[:, SMALL_FIRST:], small_dram[:, SMALL_FIRST:]).then_inc(small_in, 16)
                    for c in loads.get(h, []):
                        load_weight(c)
                    for _, b in it.stage("x_load", h):
                        if not it.l1 and not b:
                            sp.dma_start(xp_raw, xp_dram).then_inc(small_in, 16)
                            sp.dma_start(bias_raw, bias_dram).then_inc(small_in, 16)
                    for q in (L0, L1):
                        for _, b in it.stage(f"store{q}", h):
                            store_mask(q, b)
                        for m, b in it.stage(f"load{q}", h):
                            load_mask(it, q, m, b)
                    for _, b in it.stage("out_store", h):
                        sp.wait_ge(summed[L1], it.k * EXPERTS)
                        sp.dma_start(out_dram[:, bass.ds(out_at, N)], out1[:, :]).then_inc(out_stored, 16)

            run_passes(sp, body)
            for q in (L0, L1):
                sp.wait_ge(mask_stored[q], 16 * BLOCKS)
            sp.wait_ge(out_stored, 16 * BLOCKS)

        @block.tensor
        def _(pe):
            def product(out, w_h, w_l, x_h, x_l, start, stop):
                pe.matmul(out, w_h, x_h, start=start, stop=False)
                pe.matmul(out, w_l, x_h, start=False, stop=False)
                return pe.matmul(out, w_h, x_l, start=False, stop=stop)

            def expert_logits(q, tokens, block):
                for t in range(TOK):
                    mm = pe.matmul(logits[:, EXPERTS * t:EXPERTS * (t + 1)], tokens[:, D * t:D * (t + 1)],
                                   expert_gate[q], start=True, stop=True)
                mm.then_inc(logits_done[q], 1)

            def turn_mask(q, block):
                pe.wait_ge(mask_done[q], block + 1)
                for t in range(TOK):
                    mm = pe.transpose(bulk[0:EXPERTS, D * t:D * (t + 1)], mask[q][:, t, :], ident)
                mm.then_inc(turned[q], 1)

            def project(it, b):
                pe.wait_ge(x1_ready, b + 1)
                if not it.l1:
                    pe.wait_ge(xp_ready, 1)
                x1_h, x1_l = (in0_hi, in0_lo) if it.l1 else (hs_hi, hs_lo)
                for h in range(2):
                    if it.l1:
                        pe.wait_ge(gates_out, b * STEPS - HALF * (1 - h))
                    gin = gates_of(h)
                    cols = slice(h * N // 2, (h + 1) * N // 2)
                    for c in range(2):
                        pe.matmul(gin[:, :, BATCH * c:BATCH * (c + 1)], bias_pair[:, D * c:D * (c + 1)],
                                  ones_pair[:, :].unsqueeze(1).to_broadcast([2, HALF, BATCH]),
                                  start=(c == 0), stop=False)
                    for c in range(2):
                        product(gin[:, :, BATCH * c:BATCH * (c + 1)], xp_hi[:, D * c:D * (c + 1)],
                                xp_lo[:, D * c:D * (c + 1)], x1_h[:, cols], x1_l[:, cols], False, c == 1)
                if it.l1:
                    pe.wait_ge(combined[L1], it.block[L1] * GROUPS[L1] + 1)
                else:
                    pe.wait_ge(evacuated[L0], 2)
                product(bulk[:, :], xp_hi[:, 2 * D:], xp_lo[:, 2 * D:], x1_h[:, :], x1_l[:, :],
                        True, True).then_inc(xp_done, 1)

            def body(it):
                k = it.k
                for h in range(2 * it.slots):
                    i = h // 2
                    for _, b in it.stage("logits1", h):
                        if it.rec:
                            pe.wait_ge(h_done, k * STEPS)
                            if it.before == L0 and it.l0:
                                pe.wait_ge(evacuated[L0], k + 1)
                            else:
                                pe.wait_ge(evacuated[L0], BLOCKS)
                        else:
                            pe.wait_ge(h_done, k * STEPS)
                            pe.wait_ge(evacuated[L1], b)
                        expert_logits(L1, hs, b)
                    for _, b in it.stage("turn1", h):
                        if it.rec:
                            pe.wait_ge(xw_done, k + 1)
                        else:
                            pe.wait_ge(combined[L1], b * GROUPS[L1] + 1)
                        turn_mask(L1, b)
                    for _, b in it.stage("xproj", h):
                        project(it, b)
                    for _, b in it.stage("wdot", h):
                        if it.l1:
                            pe.wait_ge(evacuated[L1], k)
                        elif b:
                            pe.wait_ge(evacuated[L0], b)
                        pe.wait_ge(prod_done, b + 1)
                        pe.matmul(bulk[:, :], ones, v[:, :], start=True, stop=True).then_inc(wdot_done, 1)
                    for _, b in it.stage("gates", h):
                        pe.wait_ge(v_done, b + 1)
                        expert_logits(L0, v, b)
                    for _, b in it.stage("turn0", h):
                        pe.wait_ge(w_shifted, b + 1)
                        turn_mask(L0, b)
                    for u in it.steps("hidden", h):
                        if it.l1 or u:
                            pe.wait_ge(h_done, k * STEPS + u)
                        else:
                            pe.wait_ge(init_dve, 1)
                        h_prev = hs[:, BATCH * ((u - 1) % STEPS):BATCH * ((u - 1) % STEPS + 1)]
                        for c in range(2):
                            mm = pe.matmul(gates_of(u // HALF)[:, u % HALF, BATCH * c:BATCH * (c + 1)],
                                           rec_w[:, D * c:D * (c + 1)], h_prev, start=False, stop=True,
                                           skip_group_check=True)
                        mm.then_inc(gates_in, 1)
                        pe.matmul(mem_h[:, 0:BATCH], rec_w[:, 2 * D:], h_prev, start=True, stop=True).then_inc(mem_in, 1)
                    if h % 2 == 0 and i < it.n:
                        q, j, b = it.tile(i)
                        e, c = divmod(j, CHUNKS)
                        if j == 0:
                            pe.wait_ge(v_ready if q == L0 else hs_ready, b + 1)
                        if c == 0 and not it.rec and it.l0:
                            pe.wait_ge(w_lo, 2 * e + 1)
                        if it.any_tile(i - 2):
                            p = it.any_tile(i - 2)
                            pe.wait_ge(relu_done[p[0]], tile_count(p))
                        x_h, x_l = (in0_hi, in0_lo) if q == L0 else (hs_hi, hs_lo)
                        product(z[i % 2][:, :], first_hi[q][:, e, D * c:D * (c + 1)], first_lo[q][:, e, D * c:D * (c + 1)],
                                x_h[:, :], x_l[:, :], True, True).then_inc(z_done[q], 1)
                    if h % 2 == 1 and it.works(i) and it.tile(i - LAG):
                        t = it.tile(i - LAG)
                        q, j, b = t
                        e, c = divmod(j, CHUNKS)
                        if c == 0 and not it.rec and it.l0:
                            pe.wait_ge(w_lo, 2 * e + 2)
                        if c == 0 and i < LAG:
                            pe.wait_ge(combined[q], b * GROUPS[q] + (e - 1))
                        elif c == 0 and q == L1 and e == 0:
                            pe.wait_ge(shifted[L1], b + 1)
                        elif c == 0:
                            prev = output_before(it, q, e - q)
                            if prev:
                                pe.wait_ge(combined[prev[0]], prev[1])
                        wait_lo(pe, t)
                        product(y_bank(q, e)[:, :], second_hi[q][:, e, D * c:D * (c + 1)],
                                second_lo[q][:, e, D * c:D * (c + 1)], hid_hi[:, (i - LAG) % RING, :],
                                hid_lo[:, (i - LAG) % RING, :], c == 0, c == CHUNKS - 1).then_inc(y_done[q], 1)
                if it.rec and not it.l1:
                    pe.wait_ge(w_lo, W_ALL)

            run_passes(pe, body)

        @block.scalar
        def _(act):
            def evacuate_mask(q, block):
                act.wait_ge(turned[q], block + 1)
                act.activation(mask_t[:, :], bulk[0:EXPERTS, :], ACT.Copy).then_inc(evacuated[q], 1)

            def body(it):
                k = it.k
                weights = w_slots(it)
                for h in range(2 * it.slots):
                    i = h // 2
                    for _, b in it.stage("exp1", h):
                        act.wait_ge(shifted[L1], b + 1)
                        act.activation(g[L1][:, :, :], g[L1][:, :, :], ACT.Exp).then_inc(exp_done[L1], 1)
                    for _, b in it.stage("evac1", h):
                        if it.before == L0:
                            act.wait_ge(mask_stored[L0], 16 * (b + 2))
                        else:
                            act.wait_ge(mask_stored[L1], 16 * b)
                        evacuate_mask(L1, b)
                    for _, b in it.stage("x1_split", h):
                        act.wait_ge(summed[L0], (b + 1) * EXPERTS)
                        act.activation((in0_hi if it.l1 else hs_hi)[:, :], x1[:, :], ACT.Copy).then_inc(x1_hi, 1)
                    for _, b in it.stage("xw", h):
                        act.wait_ge(xp_done, b + 1)
                        if it.l1:
                            act.wait_ge(memory_done, b * STEPS)
                        act.activation(xw[:, :], bulk[:, :], ACT.Identity, bias=bx).then_inc(xw_done, 1)
                    for _, b in it.stage("exp_w", h):
                        act.wait_ge(w_shifted, b + 1)
                        act.activation(v[:, :], v[:, :], ACT.Exp, scale=float(D) ** -0.5).then_inc(w_exp, 1)
                    for _, b in it.stage("v_split", h):
                        act.wait_ge(v_done, b + 1)
                        if it.l1:
                            act.wait_ge(xp_done, k + 1)
                        elif it.rec:
                            act.wait_ge(z_done[L0], TILES[L0])
                        act.activation(in0_hi[:, :], v[:, :], ACT.Copy).then_inc(v_hi, 1)
                    for _, b in it.stage("exp0", h):
                        act.wait_ge(shifted[L0], b + 1)
                        act.activation(g[L0][:, :, :], g[L0][:, :, :], ACT.Exp).then_inc(exp_done[L0], 1)
                    for _, b in it.stage("evac0", h):
                        if it.l1:
                            act.wait_ge(mask_stored[L1], 16 * k)
                        elif b:
                            act.wait_ge(mask_stored[L0], 16 * b)
                        evacuate_mask(L0, b)
                    for _, b in it.stage("prepare_rec", h):
                        act.wait_ge(small_in, 48)
                        act.activation(xp_hi[:, :], xp_raw, ACT.Copy).then_inc(init_act, 1)
                        act.activation(bias_pair[:, :], bias_raw, ACT.Copy).then_inc(init_act, 1)
                        act.activation(ones_pair[:, :], ones[0:2, 0:BATCH], ACT.Copy).then_inc(init_act, 1)
                    for _, b in it.stage("copy1", h):
                        if it.l1:
                            act.wait_ge(out_stored, 16 * b)
                        act.wait_ge(summed[L0], (b + 1) * EXPERTS)
                        act.activation(out1[:, :], x1[:, :], ACT.Copy).then_inc(out1_begun, 1)
                    for u in it.steps("sigmoid", h):
                        act.wait_ge(gates_in, k * STEPS + (u + 1))
                        act.activation(th_gates[:, :], gates_of(u // HALF)[:, u % HALF, :], ACT.Tanh, scale=0.5).then_inc(gates_out, 1)
                    for u in it.steps("tanh", h):
                        act.wait_ge(memory_done, k * STEPS + (u + 1))
                        act.activation(th_mem[:, :], memory[:, :], ACT.Tanh).then_inc(th_done, 1)
                    for c in weights.get(i, []) if h % 2 == 0 else []:
                        act.wait_ge(stage_in[c % STAGE], 16 * (c // STAGE + 1))
                        q, e, hi = (L0, c // 2, (first_hi, second_hi)[c % 2]) if c < W_L0 else \
                            (L1, (c - W_L0) // 2, (first_hi, second_hi)[c % 2])
                        act.activation(hi[q][:, e, :], stage[:, c % STAGE, :], ACT.Copy).then_inc(w_hi, 1)
                    if h % 2 == 0 and i < it.n:
                        t = it.tile(i)
                        q, j, _ = t
                        if it.any_tile(i - RING):
                            wait_lo(act, it.any_tile(i - RING))
                        act.wait_ge(z_done[q], tile_count(t))
                        if q == L0 and j == 0 and not it.rec:
                            act.wait_ge(small_in, 48)
                        bias = {"bias": b1[:, j:j + 1]} if q == L0 else {}
                        act.activation(hid[:, i % RING, :], z[i % 2][:, :], ACT.Relu, **bias).then_inc(relu_done[q], 1)
                    if h % 2 == 1 and it.works(i) and it.tile(i - 1):
                        t = it.tile(i - 1)
                        if it.any_tile(i - 1 - RING):
                            p = it.any_tile(i - 1 - RING)
                            act.wait_ge(y_done[p[0]], tile_count(p))
                        act.wait_ge(relu_done[L0] if t[0] == L0 else squared, tile_count(t))
                        act.activation(hid_hi[:, (i - 1) % RING, :], hid[:, (i - 1) % RING, :], ACT.Copy).then_inc(hi_done[t[0]], 1)
                    if it.rec and h == it.hs_split:
                        act.wait_ge(h_done, (k + 1) * STEPS)
                        if it.l1:
                            act.wait_ge(z_done[L1], k * TILES[L1])
                        else:
                            act.wait_ge(xp_done, k + 1)
                        act.activation(hs_hi[:, :], hs[:, :], ACT.Copy).then_inc(hs_hi_done, 1)

            run_passes(act, body)

        @block.vector
        def _(dve):
            w_link = Chain(dve, w_chain, 3)
            link_a = {L0: Chain(dve, mask_chain_a[L0], 3), L1: Chain(dve, mask_chain_a[L1], 1)}
            link_b = {L0: Chain(dve, mask_chain_b[L0], 3), L1: Chain(dve, mask_chain_b[L1], 12)}

            def over_experts(column):
                return column.unsqueeze(2).to_broadcast([D, TOK, EXPERTS])

            def over_steps(per_step):
                return per_step.unsqueeze(2).to_broadcast([D, STEPS, BATCH])

            def prepare_rec():
                dve.wait_ge(small_in, 48)
                dve.tensor_copy(hs[:, BATCH * (STEPS - 1):], cond).then_inc(init_dve, 1)
                dve.wait_ge(init_act, 3)
                dve.tensor_tensor(xp_lo[:, :], xp_raw, xp_hi[:, :], ALU.subtract).then_inc(init_dve, 1)
                dve.tensor_tensor(bias_raw, bias_raw, bias_pair[:, :], ALU.subtract).then_inc(init_dve, 1)
                pick = small[0:2, SMALL["pick"][0]:SMALL["pick"][1]]
                dve.wait_ge(init_dve, 3)
                dve.tensor_scalar(bias_raw, bias_raw, pick[:, 1:2], None, ALU.mult).then_inc(init_dve, 1)
                dve.wait_ge(init_dve, 4)
                dve.scalar_tensor_tensor(out=bias_pair[:, :], in0=bias_pair[:, :], scalar=pick[:, 0:1], in1=bias_raw,
                                         op0=ALU.mult, op1=ALU.add).then_inc(xp_ready, 1)

            def mask0(stage, b):
                s = stat[L0]
                link = link_a[L0] if stage < 3 else link_b[L0]
                if stage == 0:
                    link.begin(b)
                    dve.wait_ge(logits_done[L0], b + 1)
                    link(dve.tensor_copy(kept[:, :, :], logits.rearrange("p (t e) -> p t e", e=EXPERTS)))
                elif stage == 1:
                    link.ready()
                    dve.tensor_reduce(s[:, 2, :], kept[:, :, :], AX.X, ALU.max)
                    for t in range(TOK):
                        last = dve.max(top[:, t, :], kept[:, t, :])
                    link(last)
                elif stage == 2:
                    link.ready()
                    dve.tensor_tensor(g[L0][:, :, :], kept[:, :, :], over_experts(s[:, 2, :]), ALU.subtract).then_inc(shifted[L0], 1)
                    link(dve.tensor_tensor(kept[:, :, :], kept[:, :, :], over_experts(top[:, :, 1]), ALU.is_ge))
                elif stage == 3:
                    link_a[L0].ready()
                    link.begin(b)
                    dve.wait_ge(exp_done[L0], b + 1)
                    link(dve.tensor_tensor(kept[:, :, :], g[L0][:, :, :], kept[:, :, :], ALU.mult))
                elif stage == 4:
                    link.ready()
                    link(dve.tensor_reduce(s[:, 0, :], kept[:, :, :], AX.X, ALU.add))
                elif stage == 5:
                    link.ready()
                    link(dve.reciprocal(s[:, 1, :], s[:, 0, :]))
                elif stage == 6:
                    link.ready()
                    dve.scalar_tensor_tensor(out=mask[L0][:, :, :], in0=kept[:, :, :], scalar=1.0 / EXPERTS,
                                             in1=over_experts(s[:, 1, :]), op0=ALU.mult, op1=ALU.mult).then_inc(mask_done[L0], 1)

            def mask1(stage, b, before):
                s = stat[L1]
                link = link_a[L1] if stage < 2 else link_b[L1]
                full = [D, TOK, EXPERTS, EXPERTS]
                other = prob[:, :, :].unsqueeze(2).to_broadcast(full)
                own = prob[:, :, :].unsqueeze(3).to_broadcast(full)
                lg = logits.rearrange("p (t e) -> p t e", e=EXPERTS)
                if stage == 0:
                    link.begin(b)
                    dve.wait_ge(logits_done[L1], b + 1)
                    link(dve.tensor_reduce(s[:, 0, :], lg, AX.X, ALU.max))
                elif stage == 1:
                    link.ready()
                    dve.tensor_tensor(g[L1][:, :, :], lg, over_experts(s[:, 0, :]), ALU.subtract).then_inc(shifted[L1], 1)
                elif stage == 2:
                    link.begin(b)
                    dve.wait_ge(exp_done[L1], b + 1)
                    link(dve.tensor_reduce(s[:, 1, :], g[L1][:, :, :], AX.X, ALU.add))
                elif stage == 3:
                    link.ready()
                    link(dve.reciprocal(s[:, 2, :], s[:, 1, :]))
                elif stage == 4:
                    link.ready()
                    link(dve.tensor_tensor(prob[:, :, :], g[L1][:, :, :], over_experts(s[:, 2, :]), ALU.mult))
                elif stage == 5:
                    if before == L0:
                        dve.wait_ge(mask_stored[L0], 16 * (b + 2))
                    else:
                        dve.wait_ge(mask_stored[L1], 16 * b)
                    link.ready()
                    link(dve.tensor_tensor(above, other, own, ALU.is_gt))
                elif stage == 6:
                    link.ready()
                    link(dve.tensor_tensor(equal, other, own, ALU.is_equal))
                elif stage == 7:
                    link.ready()
                    link(dve.tensor_tensor(equal, equal, lower.unsqueeze(1).to_broadcast(full), ALU.mult))
                elif stage == 8:
                    link.ready()
                    link(dve.tensor_tensor(above, above, equal, ALU.add))
                elif stage == 9:
                    link.ready()
                    link(dve.tensor_reduce(rank[:, :, :], above, AX.X, ALU.add))
                elif stage == 10:
                    link.ready()
                    link(dve.scalar_tensor_tensor(out=prob[:, :, :], in0=rank[:, :, :], scalar=2.0, in1=prob[:, :, :],
                                                  op0=ALU.is_lt, op1=ALU.mult))
                elif stage == 11:
                    link.ready()
                    link(dve.tensor_reduce(s[:, 3, :], prob[:, :, :], AX.X, ALU.add))
                elif stage == 12:
                    link.ready()
                    link(dve.tensor_scalar(s[:, 3, :], s[:, 3, :], 1e-9, None, ALU.max))
                elif stage == 13:
                    link.ready()
                    link(dve.reciprocal(s[:, 3, :], s[:, 3, :]))
                elif stage == 14:
                    link.ready()
                    dve.tensor_tensor(mask[L1][:, :, :], prob[:, :, :], over_experts(s[:, 3, :]), ALU.mult).then_inc(mask_done[L1], 1)

            def softmax_w(stage, b):
                link = w_link
                if stage == 0:
                    link.begin(b)
                    dve.wait_ge(wdot_done, b + 1)
                    link(dve.tensor_reduce(w_max[:, :], steps_of(bulk[:, :]), AX.X, ALU.max))
                elif stage == 1:
                    link.ready()
                    dve.tensor_tensor(steps_of(v[:, :]), steps_of(bulk[:, :]), over_steps(w_max[:, :]), ALU.subtract).then_inc(w_shifted, 1)
                elif stage == 2:
                    dve.wait_ge(w_exp, b + 1)
                    link(dve.tensor_reduce(w_sum[:, :], steps_of(v[:, :]), AX.X, ALU.add))
                elif stage == 3:
                    link.ready()
                    link(dve.reciprocal(w_inv[:, :], w_sum[:, :]))
                elif stage == 4:
                    link.ready()
                    dve.tensor_tensor(steps_of(v[:, :]), steps_of(v[:, :]), over_steps(w_inv[:, :]), ALU.mult).then_inc(v_scaled, 1)

            def combine(it, q, e, b, carried):
                dve.wait_ge(y_done[q], b * TILES[q] + CHUNKS * (e + 1))
                out_y = y_bank(q, e)[:, :]
                if q == L1 and e == 0:
                    dve.wait_ge(out1_begun, b + 1)
                    dve.tensor_tensor(out1[:, :], out_y, out1[:, :], ALU.add).then_inc(combined[L1], 1)
                    return
                m = e - q
                if m >= 2:
                    dve.wait_ge(summed[q], b * EXPERTS + (m - 1))
                else:
                    prev = term_before(it, q, m)
                    if prev:
                        dve.wait_ge(summed[prev[0]], prev[1])
                dve.wait_ge(mask_in[m % MASKS], masks_loaded(it, q, m, carried))
                if q == L0:
                    ins = dve.scalar_tensor_tensor(out=term[:, m % 2, :], in0=out_y, scalar=b2[:, e:e + 1],
                                                   in1=mask_all[:, m % MASKS, :], op0=ALU.add, op1=ALU.mult)
                else:
                    ins = dve.tensor_tensor(term[:, m % 2, :], out_y, mask_all[:, m % MASKS, :], ALU.mult)
                ins.then_inc(combined[q], 1)

            def body(it):
                k = it.k
                weights = w_slots(it)
                for h in range(2 * it.slots):
                    i = h // 2
                    for _, b in it.stage("x1_split", h):
                        x1_h, x1_l = (in0_hi, in0_lo) if it.l1 else (hs_hi, hs_lo)
                        dve.wait_ge(x1_hi, b + 1)
                        dve.tensor_tensor(x1_l[:, :], x1[:, :], x1_h[:, :], ALU.subtract).then_inc(x1_ready, 1)
                    for number, b in it.stage("mask1", h):
                        mask1(number, b, it.before)
                    for number, b in it.stage("softmax", h):
                        softmax_w(number, b)
                    for _, b in it.stage("v_split", h):
                        dve.wait_ge(v_hi, b + 1)
                        dve.tensor_tensor(in0_lo[:, :], v[:, :], in0_hi[:, :], ALU.subtract).then_inc(v_ready, 1)
                    for number, b in it.stage("mask0", h):
                        mask0(number, b)
                    for _, b in it.stage("prepare_rec", h):
                        prepare_rec()
                    for u in it.steps("memory", h):
                        n = k * STEPS + (u + 1)
                        h_prev = hs[:, BATCH * ((u - 1) % STEPS):BATCH * ((u - 1) % STEPS + 1)]
                        dve.wait_ge(mem_in, n)
                        dve.tensor_scalar(memory[:, :], mem_h[:, 0:BATCH], bh, 0.5, ALU.add, ALU.mult).then_inc(half_done, 1)
                        dve.wait_ge(gates_out, n)
                        dve.wait_ge(half_done, n)
                        dve.scalar_tensor_tensor(out=memory[:, :], in0=th_gates[:, 0:BATCH], scalar=1.0, in1=memory[:, :],
                                                 op0=ALU.add, op1=ALU.mult).then_inc(reset_done, 1)
                        dve.wait_ge(reset_done, n)
                        if u == 0:
                            dve.wait_ge(xw_done, k + 1)
                        dve.tensor_tensor(memory[:, :], memory[:, :], xw[:, BATCH * u:BATCH * (u + 1)], ALU.add).then_inc(memory_done, 1)
                        dve.tensor_scalar(keep_not[:, :], th_gates[:, BATCH:], -0.5, 0.5, ALU.mult, ALU.add)
                        dve.scalar_tensor_tensor(out=keep2[:, :], in0=th_gates[:, BATCH:], scalar=1.0, in1=h_prev,
                                                 op0=ALU.add, op1=ALU.mult).then_inc(blend_done, 1)
                    for u in it.steps("state", h):
                        n = k * STEPS + (u + 1)
                        dve.wait_ge(blend_done, n)
                        dve.wait_ge(th_done, n)
                        dve.tensor_tensor(th_mem[:, :], keep_not[:, :], th_mem[:, :], ALU.mult).then_inc(fresh_done, 1)
                        if u == 0 and it.l1:
                            dve.wait_ge(logits_done[L1], it.block[L1] + 1)
                            dve.wait_ge(hs_ready, k)
                        dve.wait_ge(fresh_done, n)
                        dve.scalar_tensor_tensor(out=hs[:, BATCH * u:BATCH * (u + 1)], in0=keep2[:, :], scalar=0.5,
                                                 in1=th_mem[:, :], op0=ALU.mult, op1=ALU.add).then_inc(h_done, 1)
                    for c in weights.get(i, []) if h % 2 == 0 else []:
                        dve.wait_ge(w_hi, c + 1)
                        q, e = (L0, c // 2) if c < W_L0 else (L1, (c - W_L0) // 2)
                        hi, lo = ((first_hi, first_lo), (second_hi, second_lo))[c % 2]
                        dve.tensor_tensor(lo[q][:, e, :], stage[:, c % STAGE, :], hi[q][:, e, :], ALU.subtract).then_inc(w_lo, 1)
                    if h % 2 == 0 and it.works(i):
                        t = it.tile(i - 1 - LAG)
                        if t and t[1] % CHUNKS == CHUNKS - 1:
                            combine(it, t[0], t[1] // CHUNKS, t[2], i - 1 - LAG < 0)
                    if h % 2 == 0 and i < it.n and it.tile(i)[0] == L1:
                        dve.wait_ge(relu_done[L1], tile_count(it.tile(i)))
                        tile = hid[:, i % RING, :]
                        dve.tensor_tensor(tile, tile, tile, ALU.mult).then_inc(squared, 1)
                    if h % 2 == 1 and it.works(i):
                        t = it.tile(i - 1)
                        if t and not lo_on_pool(*t[:2]):
                            dve.wait_ge(hi_done[t[0]], tile_count(t))
                            s = (i - 1) % RING
                            dve.tensor_tensor(hid_lo[:, s, :], hid[:, s, :], hid_hi[:, s, :], ALU.subtract).then_inc(lo_done[t[0], False], 1)
                    if it.rec and h == it.hs_split:
                        dve.wait_ge(hs_hi_done, k + 1)
                        dve.tensor_tensor(hs_lo[:, :], hs[:, :], hs_hi[:, :], ALU.subtract).then_inc(hs_ready, 1)

            run_passes(dve, body)

        @block.gpsimd
        def _(pool):
            def body(it):
                k = it.k
                for h in range(2 * it.slots):
                    i = h // 2
                    for _, b in it.stage("prod", h):
                        if it.rec or b:
                            pool.wait_ge(logits_done[L0], b)
                            pool.wait_ge(v_ready, b)
                        else:
                            pool.wait_ge(cond_in, 16)
                        pool.wait_ge(x_in, 16 * (b + 1))
                        pool.tensor_tensor(steps_of(v[:, :]), steps_of(x_t[:, :]),
                                           cond.unsqueeze(1).to_broadcast([D, STEPS, BATCH]), ALU.mult).then_inc(prod_done, 1)
                    for _, b in it.stage("v_mult", h):
                        pool.wait_ge(v_scaled, b + 1)
                        pool.tensor_tensor(v[:, :], v[:, :], x_t[:, :], ALU.mult).then_inc(v_done, 1)
                    if h % 2 == 0 and it.works(i):
                        t = it.tile(i - 1)
                        if t and lo_on_pool(*t[:2]):
                            pool.wait_ge(hi_done[t[0]], tile_count(t))
                            s = (i - 1) % RING
                            pool.tensor_tensor(hid_lo[:, s, :], hid[:, s, :], hid_hi[:, s, :], ALU.subtract).then_inc(lo_done[t[0], True], 1)
                    t = it.tile(i - 2 - LAG)
                    if h % 2 == 1 and it.works(i) and t and t[1] % CHUNKS == CHUNKS - 1 and not (t[0] == L1 and t[1] < CHUNKS):
                        q, j, b = t
                        e = j // CHUNKS
                        m = e - q
                        pool.wait_ge(combined[q], b * GROUPS[q] + (e + 1))
                        if q == L0 and m == 0:
                            if it.rec:
                                pool.wait_ge(out1_begun, k + 1)
                                pool.wait_ge(x1_ready, k + 1)
                            pool.tensor_tensor(x1[:, :], term[:, 0, :], x_t[:, :], ALU.add).then_inc(summed[L0], 1)
                        else:
                            acc = x1 if q == L0 else out1
                            if m:
                                pool.wait_ge(summed[q], b * EXPERTS + m)
                            pool.tensor_tensor(acc[:, :], term[:, m % 2, :], acc[:, :], ALU.add).then_inc(summed[q], 1)

            run_passes(pool, body)


def kernel(**inputs):
    import numpy as np
    import concourse.bacc as bacc
    from concourse.bass_utils import run_bass_kernel_spmd

    a = {n: np.asarray(v) for n, v in inputs.items()}
    x_t = np.ascontiguousarray(a["x"].transpose(2, 1, 0)).reshape(D, SEQ * BATCH)

    def second(w):
        return w.reshape(CHUNKS, D, D).transpose(1, 0, 2).reshape(D, N)

    pieces = []
    for e in range(EXPERTS):
        pieces += [a["L0_ffn_W1"][e], second(a["L0_ffn_W2"][e])]
    pieces += [a["L1_ffn_shared_fc"].T, second(a["L1_ffn_shared_proj"].T)]
    for e in range(EXPERTS):
        pieces += [a["L1_ffn_w_fc"][e].T, second(a["L1_ffn_w_proj"][e].T)]
    weights = np.ascontiguousarray(np.stack(pieces))

    small = np.zeros((D, SMALL_COLS), np.float32)

    def put(name, value, rows=D):
        lo, hi = SMALL[name]
        small[0:rows, lo:hi] = value

    put("cond", a["cond_1024"].T)
    put("b1", a["L0_ffn_b1"].reshape(EXPERTS * CHUNKS, D).T)
    put("b2", a["L0_ffn_b2"].T)
    put("bx", a["L1_cond_wx_b"].reshape(D, 1))
    put("bh", a["L1_cond_wh_b"].reshape(D, 1))
    put("gate", a["L0_ffn_W_gate"])
    put("router", a["L1_ffn_router_w"].T)
    put("rec", np.concatenate([a["L1_cond_w_W"][D:], a["L1_cond_wh_W"]], axis=1))
    put("ident", np.eye(D, dtype=np.float32))
    put("ones", 1.0)
    put("lower", np.tril(np.ones((EXPERTS, EXPERTS), np.float32), -1).reshape(1, -1))
    put("pick", np.eye(2, dtype=np.float32), rows=2)

    nc = bacc.Bacc("TRN2", target_bir_lowering=False, num_devices=1)
    arrays = {"x_in": x_t, "weights_in": weights, "small_in": small,
              "xp_in": np.concatenate([a["L1_cond_w_W"][:D], a["L1_cond_wx_W"]], axis=1),
              "gate_bias_in": np.stack([a["L1_cond_w_b"]] * 2)}
    ins = [nc.dram_tensor(n, v.shape, F32, kind="ExternalInput").ap() for n, v in arrays.items()]
    out = nc.dram_tensor("out_t", (D, SEQ * BATCH), F32, kind="ExternalOutput").ap()
    mask_dram = {q: nc.dram_tensor(f"mask_scratch{q}", (EXPERTS, N), F32, kind="Internal").ap() for q in (L0, L1)}
    build(nc, *ins, mask_dram, out)
    r = run_bass_kernel_spmd(nc, [arrays], core_ids=[0])
    got = np.asarray(r.results[0]["out_t"]).reshape(D, SEQ, BATCH)
    return np.ascontiguousarray(got.transpose(2, 1, 0))
```

```python
from contextlib import ExitStack

import concourse.bass as bass
from concourse import mybir

F32 = mybir.dt.float32
F32R = mybir.dt.float32r
ALU = mybir.AluOpType
ACT = mybir.ActivationFunctionType
AX = mybir.AxisListType

D = 128
SEQ = 128
BATCH = 32
STEPS = 16
N = STEPS * BATCH
BLOCKS = SEQ // STEPS
EXPERTS = 8
CHUNKS = 4
HALF = STEPS // 2
TOK = N // D
LAG = 4
RING = 4
L0, L1 = 0, 1
GROUPS = {L0: EXPERTS, L1: EXPERTS + 1}
TILES = {q: GROUPS[q] * CHUNKS for q in (L0, L1)}
STAGE = 2
MASKS = 4
W_L0 = 2 * GROUPS[L0]
W_ALL = 2 * (GROUPS[L0] + GROUPS[L1])

AHEAD = ("x_load", "prod", "wdot", "softmax", "exp_w", "v_mult")
PLAN = {
    "first": {
        "prod": (0, 22), "wdot": (0, 31), "softmax": ([0, 0, 0, 0, 0], [28, 29, 32, 33, 34]), "exp_w": (0, 33),
        "v_mult": (0, 34), "v_split": (0, 48), "gates": (6, 41),
        "mask0": ([4, 5, 5, 7, 7, 8, 8], [39, 41, 43, 46, 47, 48, 49]), "exp0": (6, 45), "turn0": (11, 55),
        "evac0": (10, 56), "x_load": (0, 20), "store0": (11, 56), "load0": ([12, 12, 12, 12, 19, 26, 34, 42],),
        "prepare_rec": (13,),
    },
    "second": {
        "x1_split": 12, "copy1": 22, "xproj": 16, "xw": 16, "load0": [0, 0, 1, 9, 17, 25, 33, 41],
        "rec": (17, 3, -1, -2, 0, -1, 0, -1, 1, 0), "x_load": 22, "prod": 28, "wdot": 36,
        "softmax": [37, 38, 41, 42, 43], "exp_w": 39, "v_mult": 45,
    },
    "full": {
        "logits1": 0, "exp1": 8, "mask1": [1, 2, 7, 8, 9, 10, 11, 12, 13, 15, 15, 16, 17, 18, 19], "turn1": 22,
        "evac1": 22, "x1_split": 14, "xproj": 21, "xw": 20, "prod": 100, "wdot": 108,
        "softmax": [109, 110, 113, 114, 115], "exp_w": 112, "v_mult": 117, "v_split": 47, "gates": 25,
        "mask0": [29, 30, 31, 34, 35, 36, 37], "exp0": 34, "turn0": 63, "evac0": 66, "copy1": 90, "x_load": 94,
        "store1": 25, "load1": [26, 26, 26, 26, 27, 33, 41, 57], "store0": 65,
        "load0": [66, 67, 73, 81, 89, 97, 105, 113], "out_store": 87, "rec": (22, 7.0, 0, -1, 3, 1, 0, 0, 2, 1),
    },
    "next_to_last": {
        "logits1": 0, "exp1": 3, "mask1": [0, 0, 2, 3, 4, 6, 9, 10, 11, 12, 15, 16, 17, 18, 19], "turn1": 21,
        "evac1": 21, "x1_split": 14, "xproj": 19, "xw": 19, "store1": 25, "load1": [26, 26, 26, 26, 27, 33, 41, 49],
        "out_store": 83, "rec": (21, 3.5, -1, -2, 1, -1, 0, -1, 1, -1),
    },
    "last": {
        "logits1": 4, "exp1": 4, "mask1": [1, 2, 5, 6, 7, 8, 9, 10, 11, 12, 13, 14, 15, 16, 16], "turn1": 19,
        "evac1": 19, "copy1": 9, "store1": 25, "load1": [26, 26, 26, 26, 27, 33, 41, 49], "out_store": 83,
    },
}

SMALL = {}
_at = 0
for _name, _width in (("cond", BATCH), ("ones", D), ("b1", EXPERTS * CHUNKS), ("b2", EXPERTS), ("bx", 1), ("bh", 1),
                      ("gate", EXPERTS), ("router", EXPERTS), ("rec", 3 * D), ("ident", D),
                      ("lower", EXPERTS * EXPERTS), ("gate_bias", 2)):
    SMALL[_name] = (_at, _at + _width)
    _at += _width
SMALL_COLS = _at
SMALL_FIRST = BATCH + D


def lo_on_pool(q, j):
    return j % 4 == 1 if q == L0 else j % 2 == 1


class Pass:

    def __init__(self, k, plan, l1, rec, l0, flush, before, ahead=False):
        self.k, self.l1, self.rec, self.l0 = k, l1, rec, l0
        self.flush = flush
        self.before = before
        self.carry = before is not None and plan != "last"
        self.block = {L0: k + 1, L1: k - 1}
        self.tiles = [(L1, j) for j in range(TILES[L1] if l1 else 0)] + [(L0, j) for j in range(TILES[L0] if l0 else 0)]
        self.n = len(self.tiles)
        self.at = {}
        self.ahead = ahead
        own = {name: k + 2 for name in AHEAD}
        own |= {"logits1": k - 1, "exp1": k - 1, "mask1": k - 1, "turn1": k - 1, "evac1": k - 1,
               "store1": k - 1, "load1": k - 1, "out_store": k - 1,
               "x1_split": k, "xproj": k, "xw": k, "copy1": k - 1 if plan == "last" else k}
        for name, places in PLAN[plan].items():
            if name == "rec" or (name in AHEAD and not ahead):
                continue
            blocks = (0, 1) if plan == "first" else (own.get(name, k + 1),)
            for place, block in zip(places if plan == "first" else (places,), blocks):
                for number, h in enumerate(place if isinstance(place, list) else [place]):
                    self.at.setdefault((name, h), []).append((number, block))
        self.step_of = {}
        last = 0
        if rec:
            start, stride, *later = PLAN[plan]["rec"]
            for u in range(STEPS):
                hidden = int(start + u * stride)
                offsets = later[4:8] if hidden % 2 else later[0:4]
                for part, d in zip(("hidden", "sigmoid", "memory", "tanh", "state"), [0] + offsets):
                    h = hidden + d
                    self.step_of.setdefault((part, h), []).append(u)
                    last = max(last, h)
        self.hs_split = last + 1
        if not flush and self.l1:
            self.hs_split = min(last + 1, 2 * self.n - 1)
        self.slots = max(self.n + (LAG + 3 if flush else 0), self.hs_split // 2 + 1 if rec else 0)

    def stage(self, name, h):
        return self.at.get((name, h), [])

    def steps(self, part, h):
        return self.step_of.get((part, h), [])

    def works(self, i):
        return i < self.n or self.flush

    def tile(self, i):
        if i >= self.n or (i < 0 and not self.carry):
            return None
        return self.any_tile(i)

    def any_tile(self, i):
        if i >= 0:
            q, j = self.tiles[i]
            return q, j, self.block[q]
        if self.before is None:
            return None
        return self.before, TILES[self.before] + i, (self.k if self.before == L0 else self.k - 2)


def first_passes():
    return [Pass(-1, "first", False, False, True, False, None, True),
            Pass(0, "second", False, True, True, False, L0, True)]


def loop_pass(k):
    return Pass(k, "full", True, True, True, False, L0, True)


def last_passes():
    return [Pass(BLOCKS - 2, "full", True, True, True, False, L0), Pass(BLOCKS - 1, "next_to_last", True, True, False, True, L0), Pass(BLOCKS, "last", True, False, False, True, L1)]


def run_passes(engine, body):
    for it in first_passes():
        body(it)
    with engine.Fori(1, BLOCKS - 2) as k:
        body(loop_pass(k))
    for it in last_passes():
        body(it)


def tile_count(t):
    q, j, block = t
    return block * TILES[q] + (j + 1)


def lo_count(t):
    q, j, block = t
    mine = lo_on_pool(q, j)
    per = sum(lo_on_pool(q, i) == mine for i in range(TILES[q]))
    return block * per + sum(lo_on_pool(q, i) == mine for i in range(j + 1))


def w_slots(it):
    out = {}
    if it.l0 and not it.rec:
        for c in range(W_L0):
            out.setdefault(0 if c < STAGE else 1 + CHUNKS * (c // 2 - 1) + 2 * (c % 2) - (c > 3), []).append(c)
    elif it.l0 and not it.l1:
        for c in range(W_L0, W_ALL):
            out.setdefault(1 + (c - W_L0) * (TILES[L0] - 4) // (W_ALL - W_L0), []).append(c)
    return out


def w_loads(it):
    slot = {c: i for i, cs in w_slots(it).items() for c in cs}
    out = {}
    for c in sorted(slot):
        out.setdefault(2 * slot[c - STAGE] + 1 if c - STAGE in slot else 0, []).append(c)
    return out


class Chain:

    def __init__(self, engine, sem, steps):
        self.engine, self.sem, self.steps = engine, sem, steps

    def begin(self, block):
        self.base, self.n = block * self.steps, 0

    def __call__(self, instruction):
        self.n += 1
        assert self.n <= self.steps
        instruction.then_inc(self.sem, 1)

    def ready(self):
        self.engine.wait_ge(self.sem, self.base + self.n)


def build(nc, x_dram, weights_dram, small_dram, xp_dram, mask_dram, out_dram):
    with ExitStack() as ctx:
        def sb(name, shape, dt=F32):
            return ctx.enter_context(nc.sbuf_tensor(name, shape, dt))

        def bank(name):
            return ctx.enter_context(nc.psum_tensor(name, [D, N], F32))

        def sem(name):
            return ctx.enter_context(nc.semaphore(name))

        def per_layer(name):
            return {q: sem(f"{name}{q}") for q in (L0, L1)}

        first_hi = {q: sb(f"first_hi{q}", [D, GROUPS[q], N], F32R) for q in (L0, L1)}
        first_lo = {q: sb(f"first_lo{q}", [D, GROUPS[q], N], F32R) for q in (L0, L1)}
        second_hi = {q: sb(f"second_hi{q}", [D, GROUPS[q], N], F32R) for q in (L0, L1)}
        second_lo = {q: sb(f"second_lo{q}", [D, GROUPS[q], N], F32R) for q in (L0, L1)}
        small = sb("small", [D, SMALL_COLS])
        xp_hi = sb("xp_hi", [D, 3 * D], F32R)
        xp_lo = sb("xp_lo", [D, 3 * D], F32R)
        half_bias = sb("half_bias", [D, 2])

        x_t = sb("x_t", [D, N])
        v = sb("v", [D, N])
        in0_hi = sb("in0_hi", [D, N], F32R)
        in0_lo = sb("in0_lo", [D, N], F32R)
        x1 = sb("x1", [D, N])
        hs = sb("hs", [D, N])
        hs_hi = sb("hs_hi", [D, N], F32R)
        hs_lo = sb("hs_lo", [D, N], F32R)
        xw = sb("xw", [D, N])
        out1 = sb("out1", [D, N])
        hid = sb("hid", [D, RING, N])
        hid_hi = sb("hid_hi", [D, RING, N], F32R)
        hid_lo = sb("hid_lo", [D, RING, N], F32R)
        term = sb("term", [D, 2, N])
        mask_all = sb("mask_all", [D, MASKS, N])
        compare = sb("compare", [D, N])
        mask_t = compare[0:EXPERTS, :]

        stage = sb("stage", [D, STAGE, N])
        xp_raw = xw[:, 0:3 * D]

        w_max = sb("w_max", [D, STEPS])
        w_sum = sb("w_sum", [D, STEPS])
        w_inv = sb("w_inv", [D, STEPS])
        g = {q: sb(f"g{q}", [D, TOK, EXPERTS]) for q in (L0, L1)}
        top = sb("top", [D, TOK, 8])
        kept = sb("kept", [D, TOK, EXPERTS])
        stat = {q: sb(f"stat{q}", [D, 4, TOK]) for q in (L0, L1)}
        mask = {q: sb(f"mask{q}", [D, TOK, EXPERTS]) for q in (L0, L1)}
        prob = sb("prob", [D, TOK, EXPERTS])
        rank = sb("rank", [D, TOK, EXPERTS])
        above, equal = (compare[:, N // 2 * a:N // 2 * (a + 1)].rearrange("p (t e j) -> p t e j", t=TOK, e=EXPERTS) for a in range(2))
        th_gates = sb("th_gates", [D, 2 * BATCH])
        memory = sb("memory", [D, BATCH])
        th_mem = sb("th_mem", [D, BATCH])
        keep_not = sb("keep_not", [D, BATCH])
        keep2 = sb("keep2", [D, BATCH])

        z = [bank("z0"), bank("z1")]
        y = [bank("y0"), bank("y1")]
        gate_in = [bank("gate_in0"), bank("gate_in1")]
        bulk = bank("bulk")
        mem_h = bank("mem_h")
        logits = bulk[:, 0:TOK * EXPERTS]

        def part(name):
            a, b = SMALL[name]
            return small[:, a:b]

        cond, b1, b2, ident, ones = part("cond"), part("b1"), part("b2"), part("ident"), part("ones")
        bx, bh, gate_bias, rec_w = part("bx"), part("bh"), part("gate_bias"), part("rec")
        expert_gate = {L0: part("gate"), L1: part("router")}
        lower = part("lower").rearrange("p (e j) -> p e j", e=EXPERTS)

        def steps_of(t):
            return t.rearrange("p (s b) -> p s b", b=BATCH)

        def gates_of(b):
            return gate_in[b][:, :].rearrange("p (s c) -> p s c", c=2 * BATCH)

        cond_in, small_in, x_in = sem("cond_in"), sem("small_in"), sem("x_in")
        stage_in = [sem(f"stage_in{i}") for i in range(STAGE)]
        w_hi, w_lo = sem("w_hi"), sem("w_lo")
        init_act, init_dve = sem("init_act"), sem("init_dve")
        xp_ready = sem("xp_ready")
        prod_done, wdot_done, w_shifted, w_exp = sem("prod_done"), sem("wdot_done"), sem("w_shifted"), sem("w_exp")
        w_chain, v_scaled, v_done, v_hi, v_ready = sem("w_chain"), sem("v_scaled"), sem("v_done"), sem("v_hi"), sem("v_ready")
        logits_done, shifted, exp_done = per_layer("logits_done"), per_layer("shifted"), per_layer("exp_done")
        mask_chain_a, mask_chain_b = per_layer("mask_chain_a"), per_layer("mask_chain_b")
        mask_done, turned, evacuated = per_layer("mask_done"), per_layer("turned"), per_layer("evacuated")
        mask_stored = per_layer("mask_stored")
        mask_in = [sem(f"mask_in{i}") for i in range(MASKS)]
        z_done, relu_done, hi_done, y_done = (per_layer(s) for s in ("z_done", "relu_done", "hi_done", "y_done"))
        squared = sem("squared")
        lo_done = {(q, p): sem(f"lo_done{q}{'pool' if p else 'dve'}") for q in (L0, L1) for p in (False, True)}
        combined, summed = per_layer("combined"), per_layer("summed")
        x1_hi, x1_ready, xp_done, xw_done = sem("x1_hi"), sem("x1_ready"), sem("xp_done"), sem("xw_done")
        out1_begun, out_stored = sem("out1_begun"), sem("out_stored")
        hs_hi_done, hs_ready = sem("hs_hi_done"), sem("hs_ready")
        gates_in, mem_in, half_done = sem("gates_in"), sem("mem_in"), sem("half_done")
        gates_out, keep_out = sem("gates_out"), sem("keep_out")
        reset_done, memory_done, blend_done, th_done, fresh_done = (
            sem(s) for s in ("reset_done", "memory_done", "blend_done", "th_done", "fresh_done"))
        h_done = sem("h_done")

        block = ctx.enter_context(nc.Block())

        def wait_lo(engine, t):
            engine.wait_ge(lo_done[t[0], lo_on_pool(t[0], t[1])], lo_count(t))

        def first_block(it, b):
            return not it.rec and b == 0

        def product_with_cond(engine):
            engine.tensor_tensor(steps_of(v[:, :]), steps_of(x_t[:, :]),
                                 cond.unsqueeze(1).to_broadcast([D, STEPS, BATCH]), ALU.mult).then_inc(prod_done, 1)

        def weigh_input(engine):
            engine.tensor_tensor(v[:, :], v[:, :], x_t[:, :], ALU.mult).then_inc(v_done, 1)

        def input0(b):
            return (hs_hi, hs_lo) if isinstance(b, int) and b == 1 else (in0_hi, in0_lo)

        def y_bank(q, e):
            return bulk if q == L1 and e == 0 else y[(e - q) % 2]

        def output_before(it, q, m):
            if m >= 2:
                return q, it.block[q] * GROUPS[q] + (m - 2 + q + 1)
            if q == L0 and it.l1:
                return L1, it.block[L1] * GROUPS[L1] + (GROUPS[L1] + m - 1)
            if it.before is None:
                return None
            return it.before, (it.k if it.before == L0 else it.k - 2) * GROUPS[it.before] + (GROUPS[it.before] + m - 1)

        def term_before(it, q, e):
            if e >= 2:
                return q, it.block[q] * EXPERTS + (e - 1)
            if q == L0 and it.l1:
                return L1, it.block[L1] * EXPERTS + (EXPERTS + e - 1)
            if it.before is None:
                return None
            return it.before, (it.k if it.before == L0 else it.k - 2) * EXPERTS + (EXPERTS + e - 1)

        def masks_loaded(it, q, m, carried):
            if carried:
                sets = it.k + (it.k - 1) if it.l1 else it.k
            elif q == L1:
                sets = it.block[L1] + (it.k + 1 if it.rec else BLOCKS)
            else:
                sets = it.block[L0] + (it.k if it.l1 else 0)
            return 16 * (sets * (EXPERTS // MASKS) + (m // MASKS + 1))

        def mask_before(it, q, m):
            if m >= MASKS:
                return q, it.block[q] * GROUPS[q] + (m - MASKS + q + 1)
            back = EXPERTS + m - MASKS + 1
            if q == L0 and it.l1:
                return L1, it.block[L1] * GROUPS[L1] + (back + 1)
            if it.before is None:
                return None
            if it.before == L0:
                return L0, it.k * GROUPS[L0] + back
            return L1, (it.k - 2) * GROUPS[L1] + (back + 1)

        @block.sync
        def _(sp):
            def load_weight(c):
                if c >= STAGE:
                    sp.wait_ge(w_lo, c - STAGE + 1)
                sp.dma_start(stage[:, c % STAGE, :], weights_dram[c]).then_inc(stage_in[c % STAGE], 16)

            def held(value):
                return value if isinstance(value, int) else sp.snap(value)

            def store_mask(q, b):
                if isinstance(b, int) and (q, b) == (L0, 1):
                    for sem_in in mask_in:
                        sp.wait_ge(sem_in, 16 * (EXPERTS // MASKS))
                sp.wait_ge(evacuated[q], b + 1)
                sp.dma_start(mask_dram[q], mask_t).then_inc(mask_stored[q], 16)

            def load_mask(it, q, m, b):
                prev = mask_before(it, q, m)
                if m == 0:
                    sp.wait_ge(mask_stored[q], 16 * (b + 1))
                    if it.l1:
                        prev = None
                if q == L1 and m == EXPERTS - 1 and it.l0:
                    prev = mask_before(it, L0, 0)
                if prev:
                    sp.wait_ge(combined[prev[0]], prev[1])
                row = mask_dram[q][m:m + 1, :].to_broadcast([D, N])
                sp.dma_start(mask_all[:, m % MASKS, :], row).then_inc(mask_in[m % MASKS], 16)

            def body(it):
                if it.ahead:
                    x_at = held((it.k + 2) * N)
                if it.l1:
                    out_at = held((it.k - 1) * N)
                loads = w_loads(it)
                for h in range(2 * it.slots):
                    for _, b in it.stage("x_load", h):
                        if not first_block(it, b):
                            sp.wait_ge(summed[L0], (it.k + 1) * EXPERTS + 1)
                            sp.dma_start(x_t[:, :], x_dram[:, bass.ds(x_at, N)]).then_inc(x_in, 16)
                        else:
                            sp.dma_start(small[:, 0:SMALL_FIRST], small_dram[:, 0:SMALL_FIRST]).then_inc(cond_in, 16)
                            sp.dma_start(x_t[:, :], x_dram[:, 0:N]).then_inc(x_in, 16)
                            sp.dma_start(small[:, SMALL_FIRST:], small_dram[:, SMALL_FIRST:]).then_inc(small_in, 16)
                    for c in loads.get(h, []):
                        load_weight(c)
                    for _, b in it.stage("x_load", h):
                        if first_block(it, b):
                            sp.dma_start(xp_raw, xp_dram).then_inc(small_in, 16)
                    for q in (L0, L1):
                        for _, b in it.stage(f"store{q}", h):
                            store_mask(q, b)
                        for m, b in it.stage(f"load{q}", h):
                            load_mask(it, q, m, b)
                    for _, b in it.stage("out_store", h):
                        sp.wait_ge(summed[L1], it.k * EXPERTS)
                        sp.dma_start(out_dram[:, bass.ds(out_at, N)], out1[:, :]).then_inc(out_stored, 16)

            run_passes(sp, body)
            for q in (L0, L1):
                sp.wait_ge(mask_stored[q], 16 * BLOCKS)
            sp.wait_ge(out_stored, 16 * BLOCKS)

        @block.tensor
        def _(pe):
            def product(out, w_h, w_l, x_h, x_l, start, stop):
                pe.matmul(out, w_h, x_h, start=start, stop=False)
                pe.matmul(out, w_l, x_h, start=False, stop=False)
                return pe.matmul(out, w_h, x_l, start=False, stop=stop)

            def expert_logits(q, tokens, block):
                for t in range(TOK):
                    mm = pe.matmul(logits[:, EXPERTS * t:EXPERTS * (t + 1)], tokens[:, D * t:D * (t + 1)],
                                   expert_gate[q], start=True, stop=True)
                mm.then_inc(logits_done[q], 1)

            def turn_mask(q, block):
                pe.wait_ge(mask_done[q], block + 1)
                for t in range(TOK):
                    mm = pe.transpose(bulk[0:EXPERTS, D * t:D * (t + 1)], mask[q][:, t, :], ident)
                mm.then_inc(turned[q], 1)

            def project(it, b):
                pe.wait_ge(x1_ready, b + 1)
                if not it.l1:
                    pe.wait_ge(xp_ready, 1)
                for h in range(2):
                    if it.l1:
                        pe.wait_ge(keep_out, b * STEPS - HALF * (1 - h))
                    gin = gates_of(h)
                    cols = slice(h * N // 2, (h + 1) * N // 2)
                    for c in range(2):
                        product(gin[:, :, BATCH * c:BATCH * (c + 1)], xp_hi[:, D * c:D * (c + 1)],
                                xp_lo[:, D * c:D * (c + 1)], in0_hi[:, cols], in0_lo[:, cols], c == 0, c == 1)
                if it.l1:
                    pe.wait_ge(combined[L1], it.block[L1] * GROUPS[L1] + 1)
                else:
                    pe.wait_ge(evacuated[L0], 2)
                product(bulk[:, :], xp_hi[:, 2 * D:], xp_lo[:, 2 * D:], in0_hi[:, :], in0_lo[:, :],
                        True, True).then_inc(xp_done, 1)

            def body(it):
                k = it.k
                for h in range(2 * it.slots):
                    i = h // 2
                    for _, b in it.stage("logits1", h):
                        pe.wait_ge(h_done, k * STEPS)
                        if it.before == L0 and it.l0:
                            pe.wait_ge(w_shifted, k + 2)
                        elif it.before == L0:
                            pe.wait_ge(evacuated[L0], BLOCKS)
                        else:
                            pe.wait_ge(evacuated[L1], b)
                        expert_logits(L1, hs, b)
                    for _, b in it.stage("turn1", h):
                        if it.rec:
                            pe.wait_ge(xw_done, k + 1)
                        else:
                            pe.wait_ge(combined[L1], b * GROUPS[L1] + 1)
                        turn_mask(L1, b)
                    for _, b in it.stage("xproj", h):
                        project(it, b)
                    for _, b in it.stage("wdot", h):
                        if not first_block(it, b):
                            pe.wait_ge(evacuated[L0], b)
                        if it.rec and not it.l1:
                            pe.wait_ge(xw_done, k + 1)
                        pe.wait_ge(prod_done, b + 1)
                        pe.matmul(bulk[:, :], ones, v[:, :], start=True, stop=True).then_inc(wdot_done, 1)
                    for _, b in it.stage("gates", h):
                        pe.wait_ge(v_done, b + 1)
                        if it.l1:
                            pe.wait_ge(evacuated[L1], k)
                        expert_logits(L0, v, b)
                    for _, b in it.stage("turn0", h):
                        pe.wait_ge(w_shifted, b + 1)
                        turn_mask(L0, b)
                    for u in it.steps("hidden", h):
                        if it.l1 or u:
                            pe.wait_ge(h_done, k * STEPS + u)
                        else:
                            pe.wait_ge(init_dve, 1)
                        h_prev = hs[:, BATCH * ((u - 1) % STEPS):BATCH * ((u - 1) % STEPS + 1)]
                        for c in range(2):
                            mm = pe.matmul(gates_of(u // HALF)[:, u % HALF, BATCH * c:BATCH * (c + 1)],
                                           rec_w[:, D * c:D * (c + 1)], h_prev, start=False, stop=True,
                                           skip_group_check=True)
                        mm.then_inc(gates_in, 1)
                        pe.matmul(mem_h[:, 0:BATCH], rec_w[:, 2 * D:], h_prev, start=True, stop=True).then_inc(mem_in, 1)
                    if h % 2 == 0 and i < it.n:
                        q, j, b = it.tile(i)
                        e, c = divmod(j, CHUNKS)
                        if j == 0:
                            pe.wait_ge(v_ready if q == L0 else hs_ready, b + 1)
                        if c == 0 and not it.rec and it.l0:
                            pe.wait_ge(w_lo, 2 * e + 1)
                        if it.any_tile(i - 2):
                            p = it.any_tile(i - 2)
                            pe.wait_ge(relu_done[p[0]], tile_count(p))
                        x_h, x_l = input0(b) if q == L0 else (hs_hi, hs_lo)
                        product(z[i % 2][:, :], first_hi[q][:, e, D * c:D * (c + 1)], first_lo[q][:, e, D * c:D * (c + 1)],
                                x_h[:, :], x_l[:, :], True, True).then_inc(z_done[q], 1)
                    if h % 2 == 1 and it.works(i) and it.tile(i - LAG):
                        t = it.tile(i - LAG)
                        q, j, b = t
                        e, c = divmod(j, CHUNKS)
                        if c == 0 and not it.rec and it.l0:
                            pe.wait_ge(w_lo, 2 * e + 2)
                        if c == 0 and i < LAG:
                            pe.wait_ge(combined[q], b * GROUPS[q] + (e - 1))
                        elif c == 0 and q == L1 and e == 0:
                            pe.wait_ge(shifted[L1], b + 1)
                        elif c == 0:
                            prev = output_before(it, q, e - q)
                            if prev:
                                pe.wait_ge(combined[prev[0]], prev[1])
                        wait_lo(pe, t)
                        product(y_bank(q, e)[:, :], second_hi[q][:, e, D * c:D * (c + 1)],
                                second_lo[q][:, e, D * c:D * (c + 1)], hid_hi[:, (i - LAG) % RING, :],
                                hid_lo[:, (i - LAG) % RING, :], c == 0, c == CHUNKS - 1).then_inc(y_done[q], 1)
                if it.rec and not it.l1:
                    pe.wait_ge(w_lo, W_ALL)

            run_passes(pe, body)

        @block.scalar
        def _(act):
            def evacuate_mask(q, block):
                act.wait_ge(turned[q], block + 1)
                act.activation(mask_t[:, :], bulk[0:EXPERTS, :], ACT.Copy).then_inc(evacuated[q], 1)

            def body(it):
                k = it.k
                weights = w_slots(it)
                for h in range(2 * it.slots):
                    i = h // 2
                    for c in weights.get(i, []) if h % 2 == 0 else []:
                        act.wait_ge(stage_in[c % STAGE], 16 * (c // STAGE + 1))
                        q, e, hi = (L0, c // 2, (first_hi, second_hi)[c % 2]) if c < W_L0 else \
                            (L1, (c - W_L0) // 2, (first_hi, second_hi)[c % 2])
                        act.activation(hi[q][:, e, :], stage[:, c % STAGE, :], ACT.Copy).then_inc(w_hi, 1)
                    for _, b in it.stage("exp1", h):
                        act.wait_ge(shifted[L1], b + 1)
                        act.activation(g[L1][:, :, :], g[L1][:, :, :], ACT.Exp).then_inc(exp_done[L1], 1)
                    for _, b in it.stage("evac1", h):
                        if it.before == L0:
                            act.wait_ge(mask_stored[L0], 16 * (b + 2))
                        else:
                            act.wait_ge(mask_stored[L1], 16 * b)
                        evacuate_mask(L1, b)
                    for _, b in it.stage("x1_split", h):
                        act.wait_ge(summed[L0], (b + 1) * EXPERTS)
                        act.activation(in0_hi[:, :], x1[:, :], ACT.Copy).then_inc(x1_hi, 1)
                    for _, b in it.stage("xw", h):
                        act.wait_ge(xp_done, b + 1)
                        if it.l1:
                            act.wait_ge(memory_done, b * STEPS)
                        act.activation(xw[:, :], bulk[:, :], ACT.Identity, bias=bx).then_inc(xw_done, 1)
                    for _, b in it.stage("exp_w", h):
                        act.wait_ge(w_shifted, b + 1)
                        act.activation(v[:, :], v[:, :], ACT.Exp, scale=float(D) ** -0.5).then_inc(w_exp, 1)
                    for _, b in it.stage("v_split", h):
                        act.wait_ge(v_done, b + 1)
                        if it.l1:
                            act.wait_ge(xp_done, k + 1)
                        act.activation(input0(b)[0][:, :], v[:, :], ACT.Copy).then_inc(v_hi, 1)
                    for _, b in it.stage("exp0", h):
                        act.wait_ge(shifted[L0], b + 1)
                        act.activation(g[L0][:, :, :], g[L0][:, :, :], ACT.Exp).then_inc(exp_done[L0], 1)
                    for _, b in it.stage("evac0", h):
                        if it.l1:
                            act.wait_ge(mask_stored[L1], 16 * k)
                        elif b:
                            act.wait_ge(mask_stored[L0], 16 * b)
                        evacuate_mask(L0, b)
                    for _, b in it.stage("prepare_rec", h):
                        act.wait_ge(small_in, 32)
                        act.activation(xp_hi[:, :], xp_raw, ACT.Copy).then_inc(init_act, 1)
                    for _, b in it.stage("copy1", h):
                        if it.l1:
                            act.wait_ge(out_stored, 16 * b)
                        act.wait_ge(summed[L0], (b + 1) * EXPERTS)
                        act.activation(out1[:, :], x1[:, :], ACT.Copy).then_inc(out1_begun, 1)
                    for u in it.steps("sigmoid", h):
                        act.wait_ge(gates_in, k * STEPS + (u + 1))
                        if not it.l1 and not u:
                            act.wait_ge(xp_ready, 1)
                        for c, out in enumerate((gates_out, keep_out)):
                            cols = slice(BATCH * c, BATCH * (c + 1))
                            act.activation(th_gates[:, cols], gates_of(u // HALF)[:, u % HALF, cols], ACT.Tanh,
                                           bias=half_bias[:, c:c + 1], scale=0.5).then_inc(out, 1)
                    for u in it.steps("tanh", h):
                        act.wait_ge(memory_done, k * STEPS + (u + 1))
                        act.activation(th_mem[:, :], memory[:, :], ACT.Tanh).then_inc(th_done, 1)
                    if h % 2 == 0 and i < it.n:
                        t = it.tile(i)
                        q, j, _ = t
                        if it.any_tile(i - RING):
                            wait_lo(act, it.any_tile(i - RING))
                        act.wait_ge(z_done[q], tile_count(t))
                        if q == L0 and j == 0 and not it.rec:
                            act.wait_ge(small_in, 32)
                        bias = {"bias": b1[:, j:j + 1]} if q == L0 else {}
                        act.activation(hid[:, i % RING, :], z[i % 2][:, :], ACT.Relu, **bias).then_inc(relu_done[q], 1)
                    if h % 2 == 1 and it.works(i) and it.tile(i - 1):
                        t = it.tile(i - 1)
                        if it.any_tile(i - 1 - RING):
                            p = it.any_tile(i - 1 - RING)
                            act.wait_ge(y_done[p[0]], tile_count(p))
                        act.wait_ge(relu_done[L0] if t[0] == L0 else squared, tile_count(t))
                        act.activation(hid_hi[:, (i - 1) % RING, :], hid[:, (i - 1) % RING, :], ACT.Copy).then_inc(hi_done[t[0]], 1)
                    if it.rec and h == it.hs_split:
                        act.wait_ge(h_done, (k + 1) * STEPS)
                        if it.l1:
                            act.wait_ge(z_done[L1], k * TILES[L1])
                        else:
                            act.wait_ge(z_done[L0], 2 * TILES[L0])
                        act.activation(hs_hi[:, :], hs[:, :], ACT.Copy).then_inc(hs_hi_done, 1)

            run_passes(act, body)

        @block.vector
        def _(dve):
            w_link = Chain(dve, w_chain, 3)
            link_a = {L0: Chain(dve, mask_chain_a[L0], 3), L1: Chain(dve, mask_chain_a[L1], 1)}
            link_b = {L0: Chain(dve, mask_chain_b[L0], 3), L1: Chain(dve, mask_chain_b[L1], 12)}

            def over_experts(column):
                return column.unsqueeze(2).to_broadcast([D, TOK, EXPERTS])

            def over_steps(per_step):
                return per_step.unsqueeze(2).to_broadcast([D, STEPS, BATCH])

            def prepare_rec():
                dve.wait_ge(small_in, 32)
                dve.tensor_copy(hs[:, BATCH * (STEPS - 1):], cond).then_inc(init_dve, 1)
                dve.tensor_scalar(half_bias[:, :], gate_bias, 0.5, None, ALU.mult)
                dve.wait_ge(init_act, 1)
                dve.tensor_tensor(xp_lo[:, :], xp_raw, xp_hi[:, :], ALU.subtract).then_inc(xp_ready, 1)

            def mask0(stage, b):
                s = stat[L0]
                link = link_a[L0] if stage < 3 else link_b[L0]
                if stage == 0:
                    link.begin(b)
                    dve.wait_ge(logits_done[L0], b + 1)
                    link(dve.tensor_copy(kept[:, :, :], logits.rearrange("p (t e) -> p t e", e=EXPERTS)))
                elif stage == 1:
                    link.ready()
                    dve.tensor_reduce(s[:, 2, :], kept[:, :, :], AX.X, ALU.max)
                    for t in range(TOK):
                        last = dve.max(top[:, t, :], kept[:, t, :])
                    link(last)
                elif stage == 2:
                    link.ready()
                    dve.tensor_tensor(g[L0][:, :, :], kept[:, :, :], over_experts(s[:, 2, :]), ALU.subtract).then_inc(shifted[L0], 1)
                    link(dve.tensor_tensor(kept[:, :, :], kept[:, :, :], over_experts(top[:, :, 1]), ALU.is_ge))
                elif stage == 3:
                    link_a[L0].ready()
                    link.begin(b)
                    dve.wait_ge(exp_done[L0], b + 1)
                    link(dve.tensor_tensor(kept[:, :, :], g[L0][:, :, :], kept[:, :, :], ALU.mult))
                elif stage == 4:
                    link.ready()
                    link(dve.tensor_reduce(s[:, 0, :], kept[:, :, :], AX.X, ALU.add))
                elif stage == 5:
                    link.ready()
                    link(dve.reciprocal(s[:, 1, :], s[:, 0, :]))
                elif stage == 6:
                    link.ready()
                    dve.scalar_tensor_tensor(out=mask[L0][:, :, :], in0=kept[:, :, :], scalar=1.0 / EXPERTS,
                                             in1=over_experts(s[:, 1, :]), op0=ALU.mult, op1=ALU.mult).then_inc(mask_done[L0], 1)

            def mask1(stage, b, before):
                s = stat[L1]
                link = link_a[L1] if stage < 2 else link_b[L1]
                full = [D, TOK, EXPERTS, EXPERTS]
                other = prob[:, :, :].unsqueeze(2).to_broadcast(full)
                own = prob[:, :, :].unsqueeze(3).to_broadcast(full)
                lg = logits.rearrange("p (t e) -> p t e", e=EXPERTS)
                if stage == 0:
                    link.begin(b)
                    dve.wait_ge(logits_done[L1], b + 1)
                    link(dve.tensor_reduce(s[:, 0, :], lg, AX.X, ALU.max))
                elif stage == 1:
                    link.ready()
                    dve.tensor_tensor(g[L1][:, :, :], lg, over_experts(s[:, 0, :]), ALU.subtract).then_inc(shifted[L1], 1)
                elif stage == 2:
                    link.begin(b)
                    dve.wait_ge(exp_done[L1], b + 1)
                    link(dve.tensor_reduce(s[:, 1, :], g[L1][:, :, :], AX.X, ALU.add))
                elif stage == 3:
                    link.ready()
                    link(dve.reciprocal(s[:, 2, :], s[:, 1, :]))
                elif stage == 4:
                    link.ready()
                    link(dve.tensor_tensor(prob[:, :, :], g[L1][:, :, :], over_experts(s[:, 2, :]), ALU.mult))
                elif stage == 5:
                    if before == L0:
                        dve.wait_ge(mask_stored[L0], 16 * (b + 2))
                    else:
                        dve.wait_ge(mask_stored[L1], 16 * b)
                    link.ready()
                    link(dve.tensor_tensor(above, other, own, ALU.is_gt))
                elif stage == 6:
                    link.ready()
                    link(dve.tensor_tensor(equal, other, own, ALU.is_equal))
                elif stage == 7:
                    link.ready()
                    link(dve.tensor_tensor(equal, equal, lower.unsqueeze(1).to_broadcast(full), ALU.mult))
                elif stage == 8:
                    link.ready()
                    link(dve.tensor_tensor(above, above, equal, ALU.add))
                elif stage == 9:
                    link.ready()
                    link(dve.tensor_reduce(rank[:, :, :], above, AX.X, ALU.add))
                elif stage == 10:
                    link.ready()
                    link(dve.scalar_tensor_tensor(out=prob[:, :, :], in0=rank[:, :, :], scalar=2.0, in1=prob[:, :, :],
                                                  op0=ALU.is_lt, op1=ALU.mult))
                elif stage == 11:
                    link.ready()
                    link(dve.tensor_reduce(s[:, 3, :], prob[:, :, :], AX.X, ALU.add))
                elif stage == 12:
                    link.ready()
                    link(dve.tensor_scalar(s[:, 3, :], s[:, 3, :], 1e-9, None, ALU.max))
                elif stage == 13:
                    link.ready()
                    link(dve.reciprocal(s[:, 3, :], s[:, 3, :]))
                elif stage == 14:
                    link.ready()
                    dve.tensor_tensor(mask[L1][:, :, :], prob[:, :, :], over_experts(s[:, 3, :]), ALU.mult).then_inc(mask_done[L1], 1)

            def softmax_w(stage, b):
                link = w_link
                if stage == 0:
                    link.begin(b)
                    dve.wait_ge(wdot_done, b + 1)
                    link(dve.tensor_reduce(w_max[:, :], steps_of(bulk[:, :]), AX.X, ALU.max))
                elif stage == 1:
                    link.ready()
                    dve.tensor_tensor(steps_of(v[:, :]), steps_of(bulk[:, :]), over_steps(w_max[:, :]), ALU.subtract).then_inc(w_shifted, 1)
                elif stage == 2:
                    dve.wait_ge(w_exp, b + 1)
                    link(dve.tensor_reduce(w_sum[:, :], steps_of(v[:, :]), AX.X, ALU.add))
                elif stage == 3:
                    link.ready()
                    link(dve.reciprocal(w_inv[:, :], w_sum[:, :]))
                elif stage == 4:
                    link.ready()
                    dve.tensor_tensor(steps_of(v[:, :]), steps_of(v[:, :]), over_steps(w_inv[:, :]), ALU.mult).then_inc(v_scaled, 1)

            def combine(it, q, e, b, carried):
                dve.wait_ge(y_done[q], b * TILES[q] + CHUNKS * (e + 1))
                out_y = y_bank(q, e)[:, :]
                if q == L1 and e == 0:
                    dve.wait_ge(out1_begun, b + 1)
                    dve.tensor_tensor(out1[:, :], out_y, out1[:, :], ALU.add).then_inc(combined[L1], 1)
                    return
                m = e - q
                if m >= 2:
                    dve.wait_ge(summed[q], b * EXPERTS + (m - 1))
                else:
                    prev = term_before(it, q, m)
                    if prev:
                        dve.wait_ge(summed[prev[0]], prev[1])
                dve.wait_ge(mask_in[m % MASKS], masks_loaded(it, q, m, carried))
                if q == L0:
                    ins = dve.scalar_tensor_tensor(out=term[:, m % 2, :], in0=out_y, scalar=b2[:, e:e + 1],
                                                   in1=mask_all[:, m % MASKS, :], op0=ALU.add, op1=ALU.mult)
                else:
                    ins = dve.tensor_tensor(term[:, m % 2, :], out_y, mask_all[:, m % MASKS, :], ALU.mult)
                ins.then_inc(combined[q], 1)

            def body(it):
                k = it.k
                weights = w_slots(it)
                for h in range(2 * it.slots):
                    i = h // 2
                    for _, b in it.stage("prod", h):
                        if first_block(it, b):
                            dve.wait_ge(cond_in, 16)
                            dve.wait_ge(x_in, 16)
                            product_with_cond(dve)
                    for c in weights.get(i, []) if h % 2 == 0 else []:
                        dve.wait_ge(w_hi, c + 1)
                        q, e = (L0, c // 2) if c < W_L0 else (L1, (c - W_L0) // 2)
                        hi, lo = ((first_hi, first_lo), (second_hi, second_lo))[c % 2]
                        dve.tensor_tensor(lo[q][:, e, :], stage[:, c % STAGE, :], hi[q][:, e, :], ALU.subtract).then_inc(w_lo, 1)
                    for _, b in it.stage("x1_split", h):
                        dve.wait_ge(x1_hi, b + 1)
                        dve.tensor_tensor(in0_lo[:, :], x1[:, :], in0_hi[:, :], ALU.subtract).then_inc(x1_ready, 1)
                    for number, b in it.stage("mask1", h):
                        mask1(number, b, it.before)
                    for number, b in it.stage("softmax", h):
                        softmax_w(number, b)
                    for _, b in it.stage("v_mult", h):
                        if first_block(it, b):
                            dve.wait_ge(v_scaled, 1)
                            weigh_input(dve)
                    for _, b in it.stage("v_split", h):
                        dve.wait_ge(v_hi, b + 1)
                        v_h, v_l = input0(b)
                        dve.tensor_tensor(v_l[:, :], v[:, :], v_h[:, :], ALU.subtract).then_inc(v_ready, 1)
                    for number, b in it.stage("mask0", h):
                        mask0(number, b)
                    for _, b in it.stage("prepare_rec", h):
                        prepare_rec()
                    for u in it.steps("memory", h):
                        n = k * STEPS + (u + 1)
                        h_prev = hs[:, BATCH * ((u - 1) % STEPS):BATCH * ((u - 1) % STEPS + 1)]
                        dve.wait_ge(mem_in, n)
                        dve.tensor_scalar(memory[:, :], mem_h[:, 0:BATCH], bh, 0.5, ALU.add, ALU.mult).then_inc(half_done, 1)
                        dve.wait_ge(gates_out, n)
                        dve.wait_ge(half_done, n)
                        dve.scalar_tensor_tensor(out=memory[:, :], in0=th_gates[:, 0:BATCH], scalar=1.0, in1=memory[:, :],
                                                 op0=ALU.add, op1=ALU.mult).then_inc(reset_done, 1)
                        dve.wait_ge(reset_done, n)
                        if u == 0:
                            dve.wait_ge(xw_done, k + 1)
                        dve.tensor_tensor(memory[:, :], memory[:, :], xw[:, BATCH * u:BATCH * (u + 1)], ALU.add).then_inc(memory_done, 1)
                        dve.wait_ge(keep_out, n)
                        dve.tensor_scalar(keep_not[:, :], th_gates[:, BATCH:], -0.5, 0.5, ALU.mult, ALU.add)
                        dve.scalar_tensor_tensor(out=keep2[:, :], in0=th_gates[:, BATCH:], scalar=1.0, in1=h_prev,
                                                 op0=ALU.add, op1=ALU.mult).then_inc(blend_done, 1)
                    for u in it.steps("state", h):
                        n = k * STEPS + (u + 1)
                        dve.wait_ge(blend_done, n)
                        dve.wait_ge(th_done, n)
                        dve.tensor_tensor(th_mem[:, :], keep_not[:, :], th_mem[:, :], ALU.mult).then_inc(fresh_done, 1)
                        if u == 0 and it.l1:
                            dve.wait_ge(logits_done[L1], it.block[L1] + 1)
                            dve.wait_ge(hs_ready, k)
                        dve.wait_ge(fresh_done, n)
                        dve.scalar_tensor_tensor(out=hs[:, BATCH * u:BATCH * (u + 1)], in0=keep2[:, :], scalar=0.5,
                                                 in1=th_mem[:, :], op0=ALU.mult, op1=ALU.add).then_inc(h_done, 1)
                    if h % 2 == 0 and it.works(i):
                        t = it.tile(i - 1 - LAG)
                        if t and t[1] % CHUNKS == CHUNKS - 1:
                            combine(it, t[0], t[1] // CHUNKS, t[2], i - 1 - LAG < 0)
                    if h % 2 == 0 and i < it.n and it.tile(i)[0] == L1:
                        dve.wait_ge(relu_done[L1], tile_count(it.tile(i)))
                        tile = hid[:, i % RING, :]
                        dve.tensor_tensor(tile, tile, tile, ALU.mult).then_inc(squared, 1)
                    if h % 2 == 1 and it.works(i):
                        t = it.tile(i - 1)
                        if t and not lo_on_pool(*t[:2]):
                            dve.wait_ge(hi_done[t[0]], tile_count(t))
                            s = (i - 1) % RING
                            dve.tensor_tensor(hid_lo[:, s, :], hid[:, s, :], hid_hi[:, s, :], ALU.subtract).then_inc(lo_done[t[0], False], 1)
                    if it.rec and h == it.hs_split:
                        dve.wait_ge(hs_hi_done, k + 1)
                        dve.tensor_tensor(hs_lo[:, :], hs[:, :], hs_hi[:, :], ALU.subtract).then_inc(hs_ready, 1)

            run_passes(dve, body)

        @block.gpsimd
        def _(pool):
            def body(it):
                k = it.k
                for h in range(2 * it.slots):
                    i = h // 2
                    for _, b in it.stage("prod", h):
                        if not first_block(it, b):
                            pool.wait_ge(logits_done[L0], b)
                            pool.wait_ge(v_ready, b)
                            pool.wait_ge(x_in, 16 * (b + 1))
                            product_with_cond(pool)
                    for _, b in it.stage("v_mult", h):
                        if not first_block(it, b):
                            pool.wait_ge(v_scaled, b + 1)
                            weigh_input(pool)
                    if h % 2 == 0 and it.works(i):
                        t = it.tile(i - 1)
                        if t and lo_on_pool(*t[:2]):
                            pool.wait_ge(hi_done[t[0]], tile_count(t))
                            s = (i - 1) % RING
                            pool.tensor_tensor(hid_lo[:, s, :], hid[:, s, :], hid_hi[:, s, :], ALU.subtract).then_inc(lo_done[t[0], True], 1)
                    t = it.tile(i - 2 - LAG)
                    if h % 2 == 1 and it.works(i) and t and t[1] % CHUNKS == CHUNKS - 1 and not (t[0] == L1 and t[1] < CHUNKS):
                        q, j, b = t
                        e = j // CHUNKS
                        m = e - q
                        pool.wait_ge(combined[q], b * GROUPS[q] + (e + 1))
                        if q == L0 and m == 0:
                            if it.rec:
                                pool.wait_ge(out1_begun, k + 1)
                                pool.wait_ge(x1_ready, k + 1)
                            pool.tensor_tensor(x1[:, :], term[:, 0, :], x_t[:, :], ALU.add).then_inc(summed[L0], 1)
                        else:
                            acc = x1 if q == L0 else out1
                            if m:
                                pool.wait_ge(summed[q], b * EXPERTS + m)
                            pool.tensor_tensor(acc[:, :], term[:, m % 2, :], acc[:, :], ALU.add).then_inc(summed[q], 1)

            run_passes(pool, body)


def kernel(**inputs):
    import numpy as np
    import concourse.bacc as bacc
    from concourse.bass_utils import run_bass_kernel_spmd

    a = {n: np.asarray(v) for n, v in inputs.items()}
    x_t = np.ascontiguousarray(a["x"].transpose(2, 1, 0)).reshape(D, SEQ * BATCH)

    def second(w):
        return w.reshape(CHUNKS, D, D).transpose(1, 0, 2).reshape(D, N)

    pieces = []
    for e in range(EXPERTS):
        pieces += [a["L0_ffn_W1"][e], second(a["L0_ffn_W2"][e])]
    pieces += [a["L1_ffn_shared_fc"].T, second(a["L1_ffn_shared_proj"].T)]
    for e in range(EXPERTS):
        pieces += [a["L1_ffn_w_fc"][e].T, second(a["L1_ffn_w_proj"][e].T)]
    weights = np.ascontiguousarray(np.stack(pieces))

    small = np.zeros((D, SMALL_COLS), np.float32)

    def put(name, value):
        lo, hi = SMALL[name]
        small[:, lo:hi] = value

    put("cond", a["cond_1024"].T)
    put("b1", a["L0_ffn_b1"].reshape(EXPERTS * CHUNKS, D).T)
    put("b2", a["L0_ffn_b2"].T)
    put("bx", a["L1_cond_wx_b"].reshape(D, 1))
    put("bh", a["L1_cond_wh_b"].reshape(D, 1))
    put("gate", a["L0_ffn_W_gate"])
    put("router", a["L1_ffn_router_w"].T)
    put("rec", np.concatenate([a["L1_cond_w_W"][D:], a["L1_cond_wh_W"]], axis=1))
    put("ident", np.eye(D, dtype=np.float32))
    put("ones", 1.0)
    put("lower", np.tril(np.ones((EXPERTS, EXPERTS), np.float32), -1).reshape(1, -1))
    put("gate_bias", a["L1_cond_w_b"].reshape(2, D).T)

    nc = bacc.Bacc("TRN2", target_bir_lowering=False, num_devices=1)
    arrays = {"x_in": x_t, "weights_in": weights, "small_in": small,
              "xp_in": np.concatenate([a["L1_cond_w_W"][:D], a["L1_cond_wx_W"]], axis=1)}
    ins = [nc.dram_tensor(n, v.shape, F32, kind="ExternalInput").ap() for n, v in arrays.items()]
    out = nc.dram_tensor("out_t", (D, SEQ * BATCH), F32, kind="ExternalOutput").ap()
    mask_dram = {q: nc.dram_tensor(f"mask_scratch{q}", (EXPERTS, N), F32, kind="Internal").ap() for q in (L0, L1)}
    build(nc, *ins, mask_dram, out)
    r = run_bass_kernel_spmd(nc, [arrays], core_ids=[0])
    got = np.asarray(r.results[0]["out_t"]).reshape(D, SEQ, BATCH)
    return np.ascontiguousarray(got.transpose(2, 1, 0))
```
